# Optimizing a Trainium2 kernel written in Bass

```python
import numpy as np
import jax
import jax.numpy as jnp

def _softmax(x, axis=-1):
    return jax.nn.softmax(x, axis=axis)

def _gelu(x):
    return jax.nn.gelu(x, approximate=True)

def _silu(x):
    return jax.nn.silu(x)

def _sigmoid(x):
    return jax.nn.sigmoid(x)

def _layernorm(x, axis=-1, eps=1e-05):
    m = jnp.mean(x, axis=axis, keepdims=True)
    v = jnp.var(x, axis=axis, keepdims=True)
    return (x - m) / jnp.sqrt(v + eps)

def _scatter_add(tgt, idx, src, axis=0):
    return tgt.at[idx].add(src)

def _segment_sum(src, seg, n):
    return jax.ops.segment_sum(src, seg, n)
kernel_name = 'mk_gnn_preln_d4_gnn_r8_e02252'

def setup_inputs(seed: int=0):
    np.random.seed(seed)
    _w = jnp.asarray

    def _rec_inputs():
        import jax
        import jax.numpy as jnp
        _gk = jax.random.key(seed)
        x = -0.0002117 + 1 * jax.random.normal(jax.random.fold_in(_gk, 1), (6250, 256), jnp.float32)
        src = jax.random.randint(jax.random.fold_in(_gk, 2), (100000,), 0, 6250, jnp.int32)
        dst = jnp.minimum((6250 * jax.random.uniform(jax.random.fold_in(_gk, 3), (100000,)) ** 2.0).astype(jnp.int32), 49999)
        _o = jnp.argsort(dst, stable=True)
        src = src[_o]
        dst = dst[_o]
        edge_attr_256 = 5.93493e-05 + 1.00006 * jax.random.normal(jax.random.fold_in(_gk, 11), (100000, 256), jnp.float32)
        edge_weight = jax.random.uniform(jax.random.fold_in(_gk, 13), (100000,), jnp.float32, 0.0, 0.999999)
        edge_weight1 = jax.random.uniform(jax.random.fold_in(_gk, 14), (100000, 1), jnp.float32, 0.0, 0.999999)
        return (x, src, dst, edge_attr_256, edge_weight, edge_weight1)
    x, src, dst, edge_attr_256, edge_weight, edge_weight1 = _rec_inputs()

    def _L0_gnn_setup():
        import jax, jax.numpy as jnp
        import numpy as np
        N_NODES = 12500
        N_EDGES = 200000
        HIDDEN = 256
        N_LAYERS = 2
        key = jax.random.key(seed)
        k = jax.random.split(key, 7)
        x = jax.random.normal(k[0], (N_NODES, HIDDEN), dtype=jnp.float32)
        edge_index = jax.random.randint(k[1], (2, N_EDGES), 0, N_NODES, dtype=jnp.int64)
        s = 1.0 / np.sqrt(HIDDEN)
        W = jax.random.uniform(k[2], (N_LAYERS, HIDDEN, HIDDEN), jnp.float32, -s, s)
        b = jax.random.uniform(k[3], (N_LAYERS, HIDDEN), jnp.float32, -s, s)
        resW = jax.random.uniform(k[4], (HIDDEN, HIDDEN), jnp.float32, -s, s)
        resb = jax.random.uniform(k[5], (HIDDEN,), jnp.float32, -s, s)
        return {'x': x, 'edge_index': edge_index, 'W': W, 'b': b, 'resW': resW, 'resb': resb}
    _L0_gnn_all = _L0_gnn_setup()
    _L0_gnn_in = {k: v for k, v in _L0_gnn_all.items() if k in ('W', 'b', 'resW', 'resb')}
    del _L0_gnn_all

    def _L1_gnn_setup():
        import jax, jax.numpy as jnp
        import numpy as np
        N_NODES = 12500
        N_EDGES = 200000
        D = 256
        key = jax.random.key(seed)
        ks = jax.random.split(key, 8)
        h6_all = jax.random.normal(ks[0], (N_NODES, D), dtype=jnp.float32)
        edge_index = jax.random.randint(ks[1], (2, N_EDGES), 0, N_NODES, dtype=jnp.int64)
        edge_weight = jax.random.uniform(ks[2], (N_EDGES,), dtype=jnp.float32)
        s = 1.0 / np.sqrt(D)
        W = jax.random.normal(ks[3], (D, D), dtype=jnp.float32) * s
        b = jnp.zeros((D,), dtype=jnp.float32)
        W1 = jax.random.normal(ks[4], (D, D), dtype=jnp.float32) * s
        b1 = jnp.zeros((D,), dtype=jnp.float32)
        W2 = jax.random.normal(ks[5], (D, D), dtype=jnp.float32) * s
        b2 = jnp.zeros((D,), dtype=jnp.float32)
        return {'h6_all': h6_all, 'edge_index': edge_index, 'edge_weight': edge_weight, 'W': W, 'b': b, 'W1': W1, 'b1': b1, 'W2': W2, 'b2': b2}
    _L1_gnn_all = _L1_gnn_setup()
    _L1_gnn_in = {k: v for k, v in _L1_gnn_all.items() if k in ('W', 'b', 'W1', 'b1', 'W2', 'b2')}
    del _L1_gnn_all

    def _L2_gnn_setup():
        import jax, jax.numpy as jnp
        import numpy as np
        N, E, D = (6250, 37500, 256)
        BN_EPS = 1e-05

        def _bn(z, gamma, beta, mean, var):
            return (z - mean) * jax.lax.rsqrt(var + BN_EPS) * gamma + beta
        key = jax.random.key(seed)
        ks = jax.random.split(key, 8)
        s = 1.0 / np.sqrt(D)
        return {'x': jax.random.normal(ks[0], (N, D), dtype=jnp.float32), 'edge_index': jax.random.randint(ks[1], (2, E), 0, N, dtype=jnp.int64), 'edge_attr': jax.random.normal(ks[2], (E, D), dtype=jnp.float32), 'W1': jax.random.normal(ks[3], (D, D), dtype=jnp.float32) * s, 'b1': jnp.zeros((D,), jnp.float32), 'W2': jax.random.normal(ks[4], (D, D), dtype=jnp.float32) * s, 'b2': jnp.zeros((D,), jnp.float32), 'bn1_gamma': jnp.ones((D,), jnp.float32), 'bn1_beta': jnp.zeros((D,), jnp.float32), 'bn1_mean': jnp.zeros((D,), jnp.float32), 'bn1_var': jnp.ones((D,), jnp.float32), 'bn2_gamma': jnp.ones((D,), jnp.float32), 'bn2_beta': jnp.zeros((D,), jnp.float32), 'bn2_mean': jnp.zeros((D,), jnp.float32), 'bn2_var': jnp.ones((D,), jnp.float32)}
    _L2_gnn_all = _L2_gnn_setup()
    _L2_gnn_in = {k: v for k, v in _L2_gnn_all.items() if k in ('W1', 'b1', 'W2', 'b2', 'bn1_gamma', 'bn1_beta', 'bn1_mean', 'bn1_var', 'bn2_gamma', 'bn2_beta', 'bn2_mean', 'bn2_var')}
    del _L2_gnn_all

    def _L3_gnn_setup():
        import jax, jax.numpy as jnp
        import numpy as np
        N_NODES = 6250
        N_EDGES = 100000
        DIM = 256
        key = jax.random.key(seed)
        ks = jax.random.split(key, 8)
        x = jax.random.normal(ks[0], (N_NODES, DIM), dtype=jnp.float32)
        row = jax.random.randint(ks[1], (N_EDGES,), 0, N_NODES)
        col = jax.random.randint(ks[2], (N_EDGES,), 0, N_NODES)
        col = jnp.where(col == row, (col + 1) % N_NODES, col)
        edge_index = jnp.stack([row, col]).astype(jnp.int64)
        edge_weight = jax.random.uniform(ks[3], (N_EDGES, 1), dtype=jnp.float32)
        bound = 1.0 / np.sqrt(DIM)
        W1 = jax.random.uniform(ks[4], (DIM, DIM), minval=-bound, maxval=bound, dtype=jnp.float32)
        b1 = jax.random.uniform(ks[5], (DIM,), minval=-bound, maxval=bound, dtype=jnp.float32)
        W2 = jax.random.uniform(ks[6], (DIM, DIM), minval=-bound, maxval=bound, dtype=jnp.float32)
        b2 = jax.random.uniform(ks[7], (DIM,), minval=-bound, maxval=bound, dtype=jnp.float32)
        return {'x': x, 'edge_index': edge_index, 'edge_weight': edge_weight, 'W1': W1, 'b1': b1, 'W2': W2, 'b2': b2}
    _L3_gnn_all = _L3_gnn_setup()
    _L3_gnn_in = {k: v for k, v in _L3_gnn_all.items() if k in ('W1', 'b1', 'W2', 'b2')}
    del _L3_gnn_all
    return {'x': x, 'src': src, 'dst': dst, 'edge_attr_256': edge_attr_256, 'edge_weight': edge_weight, 'edge_weight1': edge_weight1, 'L0_gnn_W': _L0_gnn_in['W'], 'L0_gnn_b': _L0_gnn_in['b'], 'L0_gnn_resW': _L0_gnn_in['resW'], 'L0_gnn_resb': _L0_gnn_in['resb'], 'L1_gnn_W': _L1_gnn_in['W'], 'L1_gnn_b': _L1_gnn_in['b'], 'L1_gnn_W1': _L1_gnn_in['W1'], 'L1_gnn_b1': _L1_gnn_in['b1'], 'L1_gnn_W2': _L1_gnn_in['W2'], 'L1_gnn_b2': _L1_gnn_in['b2'], 'L2_gnn_W1': _L2_gnn_in['W1'], 'L2_gnn_b1': _L2_gnn_in['b1'], 'L2_gnn_W2': _L2_gnn_in['W2'], 'L2_gnn_b2': _L2_gnn_in['b2'], 'L2_gnn_bn1_gamma': _L2_gnn_in['bn1_gamma'], 'L2_gnn_bn1_beta': _L2_gnn_in['bn1_beta'], 'L2_gnn_bn1_mean': _L2_gnn_in['bn1_mean'], 'L2_gnn_bn1_var': _L2_gnn_in['bn1_var'], 'L2_gnn_bn2_gamma': _L2_gnn_in['bn2_gamma'], 'L2_gnn_bn2_beta': _L2_gnn_in['bn2_beta'], 'L2_gnn_bn2_mean': _L2_gnn_in['bn2_mean'], 'L2_gnn_bn2_var': _L2_gnn_in['bn2_var'], 'L3_gnn_W1': _L3_gnn_in['W1'], 'L3_gnn_b1': _L3_gnn_in['b1'], 'L3_gnn_W2': _L3_gnn_in['W2'], 'L3_gnn_b2': _L3_gnn_in['b2']}

def reference(x, src, dst, edge_attr_256, edge_weight, edge_weight1, L0_gnn_W, L0_gnn_b, L0_gnn_resW, L0_gnn_resb, L1_gnn_W, L1_gnn_b, L1_gnn_W1, L1_gnn_b1, L1_gnn_W2, L1_gnn_b2, L2_gnn_W1, L2_gnn_b1, L2_gnn_W2, L2_gnn_b2, L2_gnn_bn1_gamma, L2_gnn_bn1_beta, L2_gnn_bn1_mean, L2_gnn_bn1_var, L2_gnn_bn2_gamma, L2_gnn_bn2_beta, L2_gnn_bn2_mean, L2_gnn_bn2_var, L3_gnn_W1, L3_gnn_b1, L3_gnn_W2, L3_gnn_b2):
    import jax
    import jax.numpy as jnp

    def _L0_gnn_ref(x, edge_index, W, b, resW, resb):
        import jax, jax.numpy as jnp
        import numpy as np
        N_NODES = 12500
        N_EDGES = 200000
        HIDDEN = 256
        N_LAYERS = 2
        N = x.shape[0]
        loop = jnp.arange(N, dtype=edge_index.dtype)
        src = jnp.concatenate([edge_index[0], loop])
        dst = jnp.concatenate([edge_index[1], loop])
        ew = jnp.ones(src.shape[0], dtype=x.dtype)
        deg = jax.ops.segment_sum(ew, dst, num_segments=N)
        dis = jnp.where(deg > 0, jax.lax.rsqrt(jnp.where(deg > 0, deg, 1.0)), 0.0)
        norm = dis[src] * ew * dis[dst]
        for l in range(W.shape[0]):
            x_res = x
            h = x @ W[l]
            msg = norm[:, None] * h[src]
            agg = jax.ops.segment_sum(msg, dst, num_segments=N) + b[l]
            x = jax.nn.relu(agg + x_res @ resW + resb)
        return x

    def _L1_gnn_ref(h6_all, edge_index, edge_weight, W, b, W1, b1, W2, b2):
        import jax, jax.numpy as jnp
        import numpy as np
        N_NODES = 12500
        N_EDGES = 200000
        D = 256
        'GCNConv(256->256, weighted, self-loops, symmetric norm) + 2-layer MLP head.'
        N = h6_all.shape[0]
        row, col = (edge_index[0], edge_index[1])
        sl = jnp.arange(N, dtype=edge_index.dtype)
        row_sl = jnp.concatenate([row, sl])
        col_sl = jnp.concatenate([col, sl])
        ew_sl = jnp.concatenate([edge_weight, jnp.ones((N,), dtype=edge_weight.dtype)])
        deg = jax.ops.segment_sum(ew_sl, row_sl, num_segments=N)
        dinv = jnp.where(deg > 0, jax.lax.rsqrt(deg), 0.0)
        norm = dinv[row_sl] * ew_sl * dinv[col_sl]
        xw = h6_all @ W
        msgs = xw[col_sl] * norm[:, None]
        h7 = jax.ops.segment_sum(msgs, row_sl, num_segments=N) + b
        h = jax.nn.relu(h7 @ W1 + b1)
        out = h @ W2 + b2
        return out

    def _L2_gnn_ref(x, edge_index, edge_attr, W1, b1, W2, b2, bn1_gamma, bn1_beta, bn1_mean, bn1_var, bn2_gamma, bn2_beta, bn2_mean, bn2_var):
        import jax, jax.numpy as jnp
        import numpy as np
        N, E, D = (6250, 37500, 256)
        BN_EPS = 1e-05

        def _bn(z, gamma, beta, mean, var):
            return (z - mean) * jax.lax.rsqrt(var + BN_EPS) * gamma + beta
        src, dst = (edge_index[0], edge_index[1])
        msg = jax.nn.relu(x[src] + edge_attr)
        agg = jax.ops.segment_sum(msg, dst, num_segments=x.shape[0])
        conv_out = x + agg
        h = x + conv_out
        f = _bn(h, bn1_gamma, bn1_beta, bn1_mean, bn1_var)
        f = jax.nn.gelu(f @ W1.T + b1, approximate=False)
        f = f @ W2.T + b2
        return _bn(h + f, bn2_gamma, bn2_beta, bn2_mean, bn2_var)

    def _L3_gnn_ref(x, edge_index, edge_weight, W1, b1, W2, b2):
        import jax, jax.numpy as jnp
        import numpy as np
        N_NODES = 6250
        N_EDGES = 100000
        DIM = 256
        n = x.shape[0]
        loops = jnp.arange(n)
        row = jnp.concatenate([edge_index[0], loops])
        col = jnp.concatenate([edge_index[1], loops])
        ew = jnp.concatenate([edge_weight, jnp.ones((n, 1), x.dtype)], axis=0)
        deg = jnp.zeros((n,), x.dtype).at[col].add(1.0)
        dinv = jnp.where(deg > 0, deg ** (-0.5), 0.0)[:, None]
        norm = dinv[row] * ew * dinv[col]

        def gcn_layer(h, W, b):
            h = h @ W.T + b
            msg = norm * h[row]
            out = jax.ops.segment_sum(msg, col, num_segments=n)
            return jax.nn.relu(out)
        h = gcn_layer(x, W1, b1)
        h = gcn_layer(h, W2, b2)
        return h
    edge_index = jnp.stack([src, dst])
    h = jnp.maximum(_layernorm(x, axis=-1), 0.0)
    x = x + _L0_gnn_ref(h, edge_index, L0_gnn_W, L0_gnn_b, L0_gnn_resW, L0_gnn_resb)
    h = jnp.maximum(_layernorm(x, axis=-1), 0.0)
    x = x + _L1_gnn_ref(h, edge_index, edge_weight, L1_gnn_W, L1_gnn_b, L1_gnn_W1, L1_gnn_b1, L1_gnn_W2, L1_gnn_b2)
    h = jnp.maximum(_layernorm(x, axis=-1), 0.0)
    x = x + _L2_gnn_ref(h, edge_index, edge_attr_256, L2_gnn_W1, L2_gnn_b1, L2_gnn_W2, L2_gnn_b2, L2_gnn_bn1_gamma, L2_gnn_bn1_beta, L2_gnn_bn1_mean, L2_gnn_bn1_var, L2_gnn_bn2_gamma, L2_gnn_bn2_beta, L2_gnn_bn2_mean, L2_gnn_bn2_var)
    h = jnp.maximum(_layernorm(x, axis=-1), 0.0)
    x = x + _L3_gnn_ref(h, edge_index, edge_weight1, L3_gnn_W1, L3_gnn_b1, L3_gnn_W2, L3_gnn_b2)
    return x

_drawn_inputs = setup_inputs


def setup_inputs(seed=0):
    import zlib

    import numpy as np

    out = dict(_drawn_inputs(seed))
    spreads = {'L1_gnn_b': (0.0, 0.1),
     'L1_gnn_b1': (0.0, 0.1),
     'L1_gnn_b2': (0.0, 0.1),
     'L2_gnn_b1': (0.0, 0.8),
     'L2_gnn_b2': (0.0, 0.8),
     'L2_gnn_bn1_gamma': (1.0, 0.2),
     'L2_gnn_bn1_beta': (0.0, 0.8),
     'L2_gnn_bn1_mean': (0.0, 0.8),
     'L2_gnn_bn1_var': (1.0, 0.2),
     'L2_gnn_bn2_gamma': (1.0, 0.2),
     'L2_gnn_bn2_beta': (0.0, 0.8),
     'L2_gnn_bn2_mean': (0.0, 0.8),
     'L2_gnn_bn2_var': (1.0, 0.2)}
    factors = {'edge_weight': 56.408,
     'edge_weight1': 8.0,
     'L0_gnn_b': 2.687,
     'L0_gnn_resb': 3.399,
     'L3_gnn_W1': 8.0,
     'L3_gnn_b1': 8.0,
     'L3_gnn_W2': 8.0,
     'L3_gnn_b2': 64.0}
    for name, (base, spread) in spreads.items():
        noise = np.random.default_rng([zlib.crc32(name.encode()), seed]).standard_normal(out[name].shape)
        drawn = base * np.exp(spread * noise) if base else spread * noise
        out[name] = jnp.asarray(drawn.astype(out[name].dtype))
    for name, factor in factors.items():
        out[name] = (out[name] * factor).astype(out[name].dtype)
    return out
```

```python
from contextlib import ExitStack

import concourse.bass as bass
from concourse import mybir

P = 128
F32 = mybir.dt.float32
BF16 = mybir.dt.bfloat16
I32 = mybir.dt.int32
U16 = mybir.dt.uint16
ALU = mybir.AluOpType
ACT = mybir.ActivationFunctionType
AX_X = mybir.AxisListType.X
EPS = 1e-5

HALF = 8
RING = 2 * HALF
BANKS = 4


class Chain:

    def __init__(self, eng, sem):
        self.eng, self.sem, self.n, self.i, self.per = eng, sem, 0, None, 0

    def __call__(self, ins):
        self.n += 1
        ins.then_inc(self.sem, 1)
        self.eng.wait_ge(self.sem, self.n if self.i is None else self.i * self.per + self.n)
        if self.i is not None:
            self.eng.nop(nofuse=True)

    def enter(self, i, per):
        self.i, self.per, self.start = i, per, self.n

    def leave(self, iterations):
        assert self.n - self.start == self.per
        self.n += self.per * (iterations - 1)
        self.i = None


def build(nc, io, out):
    N, D = io["x"].shape
    E = io["src"].shape[0]
    KC = D // P
    NB = -(-N // P)
    NB += NB % 2
    if NB * P == N:
        NB += 2
    COLS = -(-E // P)
    PAD_NODE = (NB - 1) * P
    T = (COLS * P + NB * (P - 1)) // P
    T = -(-T // RING) * RING
    GROUP = next(g for g in range(20, 0, -1) if COLS % (2 * g) == 0)
    STEPS = COLS // (2 * GROUP)
    TW = -(-T // P)
    FIELDS = 4
    LAST = E - (P - 1) * COLS
    assert (NB - 1) * P >= N and 0 < LAST <= COLS and D == KC * P

    with ExitStack() as ctx:
        def sb(name, shape, dt=F32):
            return ctx.enter_context(nc.sbuf_tensor(name, shape, dt))

        def sem(name):
            return ctx.enter_context(nc.semaphore(name))

        table = nc.dram_tensor("table", (NB * P, D), F32, kind="Internal").ap()
        records = [nc.dram_tensor(f"records{o}", (P * T, FIELDS), F32, kind="Internal").ap() for o in range(2)]
        blockrow = [nc.dram_tensor(f"blockrow{o}", (P * TW,), I32, kind="Internal").ap() for o in range(2)]

        x_all = sb("x_all", [P, NB * D])
        acc = sb("acc", [P, NB * D])
        rec = sb("rec", [P, T * FIELDS])
        row0 = sb("row0", [1, T], I32)
        gbuf = sb("gbuf", [P, RING, D])
        ebuf = sb("ebuf", [P, RING, D])
        onehot = sb("onehot", [P, RING, P])
        idx = sb("idx", [P, 2, HALF], I32)
        eidx = sb("eidx", [P, 2, HALF], I32)
        low = sb("low", [P, 2, HALF * 2])

        iota_f = sb("iota_f", [P, P])
        iota_b = sb("iota_b", [P, P], BF16)
        ident = sb("ident", [P, P])
        tri = sb("tri", [P, P])
        ones = sb("ones", [P, P])
        zero = sb("zero", [P, P])
        W = {k: sb("w_" + k, [P, KC, D]) for k in
             ("L0a", "L0b", "L0r", "L1", "L1a", "L1b", "L2a", "L2b", "L3a", "L3b")}
        rows = {k: sb("row_" + k, [P, D]) for k in
                ("L0a", "L0b", "L0r", "L1b2", "L3b1", "L3b2", "g2", "be2", "mu2", "var2", "L2b2")}
        cols = {k: sb("col_" + k, [P, KC]) for k in ("L1b", "L1b1", "L2b1", "g1", "be1", "mu1", "var1")}
        stats = sb("stats", [P, NB * 6])
        mean, rstd = sb("mean", [P, NB]), sb("rstd", [P, NB])
        tmpa, tmpb = sb("tmpa", [P, NB]), sb("tmpb", [P, NB])
        dis, sq, diw = sb("dis", [P, NB]), sb("sq", [P, NB]), sb("diw", [P, NB])

        tin = sb("tin", [P, 2, D])
        opa, opb = sb("opa", [P, 2, D]), sb("opb", [P, 2, D])
        opT = sb("opT", [P, 2, 2 * D])
        root_v, root_r, root_t = opT[:, 0, 0:D], opT[:, 0, D:2 * D], opT[:, 1, 0:D]
        mid1, mid2 = opb, tin
        fin = sb("fin", [P, 2, D])

        arena = {"at": 0}

        def carve(words, dt=F32):
            a = acc[:, arena["at"]:arena["at"] + words]
            arena["at"] += words
            assert arena["at"] <= NB * D
            return a if dt == F32 else a.bitcast(dt)

        keys_i = [carve(COLS, I32) for _ in range(2)]
        weight = [carve(COLS) for _ in range(2)]
        srec = carve(COLS * FIELDS).rearrange("p (c f) -> p c f", f=FIELDS)
        low_f, high_f = carve(COLS), carve(COLS)
        work_i = carve(COLS, I32)
        place = carve(COLS)
        place_i = carve(COLS, I32)
        maskw = -(-COLS // 2)
        masks = [carve(maskw, BF16)[:, 0:COLS] for _ in range(2)]
        high_b = carve(maskw, BF16)[:, 0:COLS]
        onehot_flat = onehot[:].rearrange("p r n -> p (r n)")
        scans = [onehot_flat[:, k * COLS:(k + 1) * COLS] for k in range(2)]
        ebuf_flat = ebuf[:].rearrange("p r d -> p (r d)")
        gbuf_flat = gbuf[:].rearrange("p r d -> p (r d)")
        oh_low = [gbuf_flat[:, 0:GROUP * P], x_all[:, 0:GROUP * P]]
        oh_high = [ebuf_flat[:, k * GROUP * NB:(k + 1) * GROUP * NB] for k in range(2)]
        cnt = ebuf_flat[:, 2 * GROUP * NB:2 * GROUP * NB + NB]
        small = [ebuf_flat[:, 2 * GROUP * NB + (k + 1) * NB:2 * GROUP * NB + (k + 2) * NB] for k in range(5)]
        base_at = 2 * GROUP * NB + 6 * NB
        blk_cmp = x_all[:, GROUP * P:GROUP * P + TW * NB]
        blk_f = x_all[:, GROUP * P + TW * NB:GROUP * P + TW * NB + TW]
        blk_i = [ebuf_flat[:, base_at + o * TW:base_at + (o + 1) * TW].bitcast(I32) for o in range(2)]
        tile_no = ebuf_flat[:, base_at + 2 * TW:base_at + 3 * TW]
        assert base_at + 3 * TW <= RING * D and GROUP * P <= RING * D
        stage_idx = sb("stage_idx", [P, 2, GROUP], I32)
        stage_rec = sb("stage_rec", [P, 2, GROUP * FIELDS])

        bank = [ctx.enter_context(nc.psum_tensor(f"bank{k}", [P, 512], F32)) for k in range(8)]

        s_pads, s_iota, s_unfilled, s_xfree = (sem(k) for k in ("pads_written", "constants_ready", "unfilled_ready", "x_free"))
        s_deg = sem("degrees_ready")
        s_edges, s_nodes, s_params = sem("edges_loaded"), sem("nodes_loaded"), sem("params_loaded")
        s_chain, s_pchain = sem("vector_chain"), sem("pool_chain")
        s_root_in, s_root_out = sem("root_asked"), sem("root_taken")
        s_oh, s_ohused = sem("degree_onehots_ready"), sem("degree_onehots_used")
        s_cnt, s_off = sem("counts_ready"), sem("offsets_ready")
        s_prefill, s_place = sem("records_prefilled"), sem("places_ready")
        s_blk, s_blkst = sem("blocks_ready"), sem("blocks_stored")
        s_stage, s_scat = sem("scatter_staged"), [sem(f"scattered{k}") for k in range(2)]
        s_recld = sem("records_loaded")
        s_staged = sem("indices_staged")
        s_gath = [sem(f"gathered{k}") for k in range(RING)]
        s_egath = [sem(f"edges_gathered{k}") for k in range(RING)]
        s_msg, s_relu = sem("messages_added"), sem("messages_ready")
        s_onehot, s_tile, s_added = sem("onehot_ready"), sem("tile_summed"), sem("tile_added")
        s_z, s_row = sem("normalized"), sem("table_rows_ready")
        s_tabst = sem("table_stored")
        s_tin = [sem(f"table_block{k}_loaded") for k in range(2)]
        s_op, s_turn, s_turned = sem("operands_ready"), sem("operands_turned"), sem("turned_copied")
        s_m1, s_m1o = sem("first_product"), sem("first_copied")
        s_m2, s_m2o = sem("second_product"), sem("second_copied")
        s_pf, s_done = sem("last_product"), sem("block_done")
        s_out = sem("output_stored")

        PASSES = [(0, False, False), (0, False, False), (1, True, False),
                  (0, False, True), (0, True, False), (0, True, False)]
        DENSE = ["gcn0", "gcn1", "mlp", "gine", "lin1", "lin2", "last"]
        READS_TABLE = ["gcn0", "gcn1", "gine"]
        FIRST_MID = ["mlp", "gine"]
        ITER = T // RING
        BI = NB // 2

        def blk(t, b):
            return t[:, bass.ds(b * D, D)]

        block = ctx.enter_context(nc.Block())

        @block.sync
        def _(sp):
            sp.wait_ge(s_pads, 1)
            for dst_t, a in ((keys_i[0], io["src"]), (keys_i[1], io["dst"]),
                             (weight[0], io["edge_weight1"].rearrange("e a -> (e a)")), (weight[1], io["edge_weight"])):
                sp.dma_start(dst_t[0:P - 1, :], a[0:(P - 1) * COLS].rearrange("(p c) -> p c", c=COLS)).then_inc(s_edges, 16)
                sp.dma_start(dst_t[P - 1:P, 0:LAST], a[(P - 1) * COLS:E].rearrange("(p c) -> p c", p=1)).then_inc(s_edges, 16)
            sp.wait_ge(s_unfilled, 1)
            for o in range(2):
                sp.dma_start(records[o].rearrange("(p t) f -> p (t f)", p=P), rec[:]).then_inc(s_prefill, 16)
            for k, a in (("L0a", io["L0_gnn_W"][0]), ("L0b", io["L0_gnn_W"][1]), ("L0r", io["L0_gnn_resW"]),
                         ("L1", io["L1_gnn_W"]), ("L1a", io["L1_gnn_W1"]), ("L1b", io["L1_gnn_W2"]),
                         ("L2a", io["L2_gnn_W1"]), ("L2b", io["L2_gnn_W2"]),
                         ("L3a", io["L3_gnn_W1"]), ("L3b", io["L3_gnn_W2"])):
                sp.dma_start(W[k][:], a.rearrange("(k p) n -> p k n", p=P)).then_inc(s_params, 16)
            for k, a in (("L0a", io["L0_gnn_b"][0]), ("L0b", io["L0_gnn_b"][1]), ("L0r", io["L0_gnn_resb"]),
                         ("L1b2", io["L1_gnn_b2"]), ("L3b1", io["L3_gnn_b1"]), ("L3b2", io["L3_gnn_b2"]),
                         ("g2", io["L2_gnn_bn2_gamma"]), ("be2", io["L2_gnn_bn2_beta"]), ("mu2", io["L2_gnn_bn2_mean"]),
                         ("var2", io["L2_gnn_bn2_var"]), ("L2b2", io["L2_gnn_b2"])):
                sp.dma_start(rows[k][:], a.partition_broadcast(P)).then_inc(s_params, 16)
            with nc.allow_non_contiguous_dma(reason="seven vectors of 256, one element per partition"):
                for k, a in (("L1b", io["L1_gnn_b"]), ("L1b1", io["L1_gnn_b1"]), ("L2b1", io["L2_gnn_b1"]),
                             ("g1", io["L2_gnn_bn1_gamma"]), ("be1", io["L2_gnn_bn1_beta"]),
                             ("mu1", io["L2_gnn_bn1_mean"]), ("var1", io["L2_gnn_bn1_var"])):
                    sp.dma_start(cols[k][:], a.rearrange("(m p) -> p m", p=P)).then_inc(s_params, 16)
            for o in range(2):
                sp.wait_ge(s_blk, o + 1)
                sp.dma_start(blockrow[o].rearrange("(p t) -> p t", p=P), blk_i[o]).then_inc(s_blkst, 16)
            sp.wait_ge(s_xfree, 1)
            full = N // P
            sp.dma_start(x_all[:, 0:full * D].rearrange("p (b d) -> p b d", d=D),
                         io["x"][0:full * P].rearrange("(b p) d -> p b d", p=P)).then_inc(s_nodes, 16)
            if N % P:
                sp.dma_start(x_all[0:N % P, full * D:(full + 1) * D], io["x"][full * P:N]).then_inc(s_nodes, 16)

            table_b = table.rearrange("(b p) d -> p b d", p=P)

            def load_records(m):
                o = PASSES[m][0]
                if m in (0, 2):
                    if m == 0:
                        for k in range(2):
                            sp.wait_ge(s_scat[k], 2 * 16 * GROUP * STEPS)
                        sp.wait_ge(s_blkst, 32)
                    sp.dma_start(rec[:], records[o].rearrange("(p t) f -> p (t f)", p=P)).then_inc(s_recld, 16)
                    sp.dma_start(row0[:], blockrow[o][0:T].rearrange("(p t) -> p t", p=1)).then_inc(s_recld, 16)
                elif m == 3:
                    sp.dma_start(rec[:], records[0].rearrange("(p t) f -> p (t f)", p=P)).then_inc(s_recld, 16)
                    sp.dma_start(row0[:], blockrow[0][0:T].rearrange("(p t) -> p t", p=1)).then_inc(s_recld, 16)

            def store_table(made, per_block):
                sp.wait_ge(made, per_block + NB)
                sp.dma_start(table_b, acc[:].rearrange("p (b d) -> p b d", d=D)).then_inc(s_tabst, 16)

            def read_table(q):
                r = READS_TABLE.index(DENSE[q])
                sp.wait_ge(s_tabst, 16 * (1 + [0, 1, 3][r]))
                with sp.Fori(0, BI) as i:
                    for j in range(2):
                        sp.wait_ge(s_op, i * 2 + (NB * q + j + 1))
                        sp.dma_start(tin[:, j, :], table_b[:, bass.ds(i * 2 + j, 1), :].rearrange("p b d -> p (b d)")
                                     ).then_inc(s_tin[j], 16)

            load_records(0)
            store_table(s_row, 2)
            read_table(0)
            store_table(s_done, 2)
            read_table(1)
            store_table(s_row, 2 + NB)
            load_records(2)
            store_table(s_row, 2 + 2 * NB)
            load_records(3)
            read_table(3)
            store_table(s_done, 2 + 4 * NB)
            store_table(s_done, 2 + 5 * NB)
            sp.wait_ge(s_done, 2 + 7 * NB)
            sp.dma_start(out[0:full * P].rearrange("(b p) d -> p b d", p=P),
                         x_all[:, 0:full * D].rearrange("p (b d) -> p b d", d=D)).then_inc(s_out, 16)
            if N % P:
                sp.dma_start(out[full * P:N], x_all[0:N % P, full * D:(full + 1) * D]).then_inc(s_out, 16)
            sp.wait_ge(s_out, 32 if N % P else 16)

        @block.gpsimd
        def _(pool):
            link = Chain(pool, s_pchain)
            nc.gpsimd.iota(iota_f[:], pattern=[[1, P]], base=0, channel_multiplier=0,
                           allow_small_or_imprecise_dtypes=True)
            nc.gpsimd.iota(tile_no, pattern=[[1, TW]], base=0, channel_multiplier=TW,
                           allow_small_or_imprecise_dtypes=True)
            link(nc.gpsimd.memset(ident[:], 0.0))
            link(nc.gpsimd.affine_select(out=ident[:], in_=ident[:], compare_op=ALU.not_equal, fill=1.0, base=0,
                                         pattern=[[-1, P]], channel_multiplier=1))
            link(nc.gpsimd.memset(tri[:], 0.0))
            link(nc.gpsimd.affine_select(out=tri[:], in_=tri[:], compare_op=ALU.is_ge, fill=1.0, base=0,
                                         pattern=[[-1, P]], channel_multiplier=1))
            nc.gpsimd.iota(place_i, pattern=[[1, COLS]], base=0, channel_multiplier=COLS).then_inc(s_iota, 1)

            for o in range(2):
                pool.wait_ge(s_prefill, 32)
                with pool.Fori(0, STEPS) as i:
                    for h in range(2):
                        pool.wait_ge(s_stage, i * 2 + (2 * STEPS * o + h + 1))
                        pool.nop(nofuse=True)
                        for u in range(GROUP):
                            nc.gpsimd.indirect_dma_start(
                                out=records[o][:, :], out_offset=bass.IndirectOffsetOnAxis(ap=stage_idx[:, h, u:u + 1], axis=0),
                                in_=stage_rec[:, h, u * FIELDS:(u + 1) * FIELDS], in_offset=None).then_inc(s_scat[h], 16)

            for m, (o, weighted, attrs) in enumerate(PASSES):
                pool.wait_ge(s_tabst, 16 * (m + 1))
                with pool.Fori(0, ITER) as i:
                    for h in range(2):
                        pool.wait_ge(s_staged, i * 2 + (2 * ITER * m + h + 1))
                        for u in range(HALF):
                            k = h * HALF + u
                            pool.wait_ge(s_tile, i * RING + (T * m + k + 1))
                            pool.nop(nofuse=True)
                            nc.gpsimd.indirect_dma_start(
                                out=gbuf[:, k, :], out_offset=None, in_=table[:, :],
                                in_offset=bass.IndirectOffsetOnAxis(ap=idx[:, h, u:u + 1], axis=0)).then_inc(s_gath[k], 16)
                            if attrs:
                                nc.gpsimd.indirect_dma_start(
                                    out=ebuf[:, k, :], out_offset=None, in_=io["edge_attr_256"][:, :],
                                    in_offset=bass.IndirectOffsetOnAxis(ap=eidx[:, h, u:u + 1], axis=0)).then_inc(s_egath[k], 16)

        @block.scalar
        def _(act):
            roots = [0]

            def root(v, r):
                roots[0] += 1
                act.wait_ge(s_root_in, roots[0])
                nc.scalar.activation(r, v, ACT.Sqrt).then_inc(s_root_out, 1)

            def stage(i, o, h):
                nc.scalar.copy(stage_idx[:, h, :], place_i[:, bass.ds(i * (2 * GROUP) + h * GROUP, GROUP)])
                src = srec.rearrange("p c f -> p (c f)")
                nc.scalar.copy(stage_rec[:, h, :], src[:, bass.ds(i * (2 * GROUP * FIELDS) + h * GROUP * FIELDS, GROUP * FIELDS)]
                               ).then_inc(s_stage, 1)

            for o in range(2):
                act.wait_ge(s_place, o + 1)
                for h in range(2):
                    if o:
                        act.wait_ge(s_scat[h], 16 * GROUP * STEPS * o)
                    stage(0, o, h)
                with act.Fori(1, STEPS) as i:
                    for h in range(2):
                        act.wait_ge(s_scat[h], i * (16 * GROUP) + 16 * GROUP * STEPS * o)
                        act.nop(nofuse=True)
                        stage(i, o, h)

            root(root_v[:, 0:NB], root_r[:, 0:NB])
            root(root_v[:, 0:NB], root_r[:, 0:NB])
            root(root_v[:, 0:KC], root_r[:, 0:KC])
            root(root_v, root_r)

            def edge_pass(m):
                o, weighted, attrs = PASSES[m]
                act.wait_ge(s_recld, 32 * [1, 1, 2, 3, 3, 3][m])
                recs = rec[:].rearrange("p (t f) -> p t f", f=FIELDS)
                with act.Fori(0, ITER) as i:
                    for h in range(2):
                        act.wait_ge(s_tile, i * RING + (T * m + HALF * (h + 1)))
                        act.nop(nofuse=True)
                        at = bass.ds(i * RING + h * HALF, HALF)
                        nc.scalar.copy(idx[:, h, :], recs[:, at, 0])
                        if attrs:
                            nc.scalar.copy(eidx[:, h, :], recs[:, at, 3])
                        nc.scalar.copy(low[:, h, :].rearrange("p (t f) -> p t f", f=2), recs[:, at, 1:3]).then_inc(s_staged, 1)
                        if attrs:
                            for u in range(HALF):
                                k = h * HALF + u
                                act.wait_ge(s_msg, i * RING + (k + 1))
                                nc.scalar.activation(gbuf[:, k, :], gbuf[:, k, :], ACT.Relu).then_inc(s_relu, 1)

            norms = [0]

            def norm(scale, made):
                root(root_v[:, 0:NB], root_r[:, 0:NB])
                with act.Fori(0, BI) as i:
                    for j in range(2):
                        act.wait_ge(s_z, i * 2 + (NB * made + j + 1))
                        act.nop(nofuse=True)
                        b = i * 2 + j
                        nc.scalar.activation(blk(acc, b), opa[:, j, :], ACT.Relu,
                                             scale=1.0 if scale is None else scale[:, bass.ds(b, 1)]).then_inc(s_row, 1)

            def dense(q):
                kind = DENSE[q]
                if kind == "last":
                    return
                n = NB * q
                two = kind in ("gcn0", "gcn1")
                with act.Fori(0, BI) as i:
                    for j in range(2):
                        act.wait_ge(s_turn, i * 2 + (n + j + 1))
                        width = 2 * D if two else D
                        if kind == "gine":
                            for c in range(KC):
                                ins = nc.scalar.activation(opT[:, j, c * P:(c + 1) * P], bank[4 + j][:, c * P:(c + 1) * P], ACT.Identity,
                                                           bias=cols["be1"][:, c:c + 1], scale=cols["g1"][:, c:c + 1])
                        elif kind == "lin1":
                            ins = nc.scalar.activation(opT[:, j, 0:width], bank[4 + j][:, 0:width], ACT.Relu)
                        else:
                            ins = nc.scalar.activation(opT[:, j, 0:width], bank[4 + j][:, 0:width], ACT.Copy)
                        ins.then_inc(s_turned, 1)
                    if kind in FIRST_MID:
                        f = FIRST_MID.index(kind)
                        func, b = (ACT.Identity, "L1b") if kind == "mlp" else (ACT.Gelu, "L2b1")
                        for j in range(2):
                            act.wait_ge(s_m1, i * 2 + (NB * f + j + 1))
                            for c in range(KC):
                                ins = nc.scalar.activation(mid1[:, j, c * P:(c + 1) * P], bank[6 + j][:, c * P:(c + 1) * P], func,
                                                           bias=cols[b][:, c:c + 1])
                            ins.then_inc(s_m1o, 1)
                    if kind == "mlp":
                        for j in range(2):
                            act.wait_ge(s_m2, i * 2 + (j + 1))
                            for c in range(KC):
                                ins = nc.scalar.activation(mid2[:, j, c * P:(c + 1) * P], bank[2 + j][:, c * P:(c + 1) * P], ACT.Relu,
                                                           bias=cols["L1b1"][:, c:c + 1])
                            ins.then_inc(s_m2o, 1)

            norm(dis, 0)
            edge_pass(0)
            dense(0)
            edge_pass(1)
            dense(1)
            norm(diw, 1)
            edge_pass(2)
            dense(2)
            norm(None, 2)
            edge_pass(3)
            dense(3)
            root(root_v[:, 0:NB], root_r[:, 0:NB])
            dense(4)
            edge_pass(4)
            dense(5)
            edge_pass(5)

        @block.tensor
        def _(pe):
            for o in range(2):
                if o:
                    pe.wait_ge(s_cnt, o)
                else:
                    pe.wait_ge(s_iota, 1)
                    pe.wait_ge(s_pads, 1)
                nc.tensor.matmul(bank[0][:, 0:NB], zero[:], zero[:, 0:NB], start=True, stop=False, skip_group_check=True)
                with pe.Fori(0, STEPS) as i:
                    for h in range(2):
                        pe.wait_ge(s_oh, i * 2 + (2 * STEPS * o + h + 1))
                        for u in range(GROUP):
                            ins = nc.tensor.matmul(bank[0][:, 0:NB], oh_low[h][:, u * P:(u + 1) * P],
                                                   oh_high[h][:, u * NB:(u + 1) * NB],
                                                   start=False, stop=False, skip_group_check=True)
                        ins.then_inc(s_ohused, 1)
                nc.tensor.matmul(bank[0][:, 0:NB], zero[:], zero[:, 0:NB], start=False, stop=True,
                                 skip_group_check=True).then_inc(s_deg, 1)
                pe.wait_ge(s_cnt, o + 1)
                nc.tensor.matmul(bank[2][:, 0:NB], tri[:], cnt, start=True, stop=True)
                nc.tensor.matmul(bank[2][:, NB:2 * NB], ones[:], cnt, start=True, stop=True).then_inc(s_off, 1)

            def edge_pass(m):
                o, weighted, attrs = PASSES[m]
                with pe.Fori(0, ITER) as i:
                    for k in range(RING):
                        pe.wait_ge(s_onehot, i * RING + (T * m + k + 1))
                        if attrs:
                            pe.wait_ge(s_relu, i * RING + (k + 1))
                        else:
                            pe.wait_ge(s_gath[k], i * 16 + 16 * (ITER * m + 1))
                        pe.wait_ge(s_added, i * RING + (T * m + k + 1))
                        nc.tensor.matmul(bank[k % BANKS][:, 0:D], onehot[:, k, :], gbuf[:, k, :],
                                         start=True, stop=True).then_inc(s_tile, 1)

            def dense(q):
                kind = DENSE[q]
                if kind == "last":
                    return
                n = NB * q
                two = kind in ("gcn0", "gcn1")
                wa, wb, wc = {"gcn0": ("L0a", "L0r", None), "gcn1": ("L0b", "L0r", None), "mlp": ("L1b", "L1", "L1a"),
                              "gine": ("L2b", "L2a", None), "lin1": ("L3a", None, None), "lin2": ("L3b", None, None)}[kind]

                def middle(to, w, of):
                    for m_ in range(KC):
                        for k in range(KC):
                            ins = nc.tensor.matmul(to[:, m_ * P:(m_ + 1) * P], W[w][:, k, m_ * P:(m_ + 1) * P],
                                                   of[:, k * P:(k + 1) * P], start=(k == 0), stop=(k == KC - 1))
                    return ins

                with pe.Fori(0, BI) as i:
                    for j in range(2):
                        pe.wait_ge(s_op, i * 2 + (n + j + 1 + 2))
                        parts = [opa, opb] if two else [opa]
                        for s, t in enumerate(parts):
                            for c in range(KC):
                                at = (s * KC + c) * P
                                ins = nc.tensor.transpose(bank[4 + j][:, at:at + P], t[:, j, c * P:(c + 1) * P], ident[:])
                        ins.then_inc(s_turn, 1)
                    src = opT
                    if kind in FIRST_MID:
                        f = FIRST_MID.index(kind)
                        for j in range(2):
                            pe.wait_ge(s_turned, i * 2 + (n + j + 1))
                            middle(bank[6 + j], wb, opT[:, j, :]).then_inc(s_m1, 1)
                        src = mid1
                    if kind == "mlp":
                        for j in range(2):
                            pe.wait_ge(s_m1o, i * 2 + (j + 1))
                            middle(bank[2 + j], wc, mid1[:, j, :]).then_inc(s_m2, 1)
                        src = mid2
                    for j in range(2):
                        if kind == "mlp":
                            pe.wait_ge(s_m2o, i * 2 + (j + 1))
                        elif kind in FIRST_MID:
                            pe.wait_ge(s_m1o, i * 2 + (NB * f + j + 1))
                        else:
                            pe.wait_ge(s_turned, i * 2 + (n + j + 1))
                        ws = [wa, wb] if two else [wa]
                        for s, w in enumerate(ws):
                            for k in range(KC):
                                at = (s * KC + k) * P
                                ins = nc.tensor.matmul(bank[j][:, 0:D], src[:, j, at:at + P], W[w][:, k, :],
                                                       start=(s == 0 and k == 0), stop=(s == len(ws) - 1 and k == KC - 1))
                        ins.then_inc(s_pf, 1)

            pe.wait_ge(s_params, 16 * 28)
            edge_pass(0)
            dense(0)
            edge_pass(1)
            dense(1)
            edge_pass(2)
            dense(2)
            edge_pass(3)
            dense(3)
            dense(4)
            edge_pass(4)
            dense(5)
            edge_pass(5)

        @block.vector
        def _(dve):
            link = Chain(dve, s_chain)
            V = nc.vector
            roots = [0]

            V.memset(zero[:], 0.0)
            for t in keys_i:
                V.memset(t[96:P, :], PAD_NODE)
            V.memset(weight[0][96:P, :], 0.0)
            V.memset(weight[1][96:P, :], 0.0).then_inc(s_pads, 1)
            r3 = rec[:].rearrange("p (t f) -> p t f", f=FIELDS)
            link(V.memset(rec[:], 0.0))
            V.memset(r3[:, :, 1:2], -1.0).then_inc(s_unfilled, 1)
            V.memset(ones[:], 1.0).then_inc(s_ohused, 2)
            V.memset(onehot[:], 0.0).then_inc(s_tile, RING)
            V.memset(tmpa[:], 0.0).then_inc(s_added, BANKS)
            V.memset(tmpb[:], 0.0).then_inc(s_row, 2)
            V.memset(mean[:], 0.0).then_inc(s_op, 2)
            V.memset(rstd[:], 0.0).then_inc(s_done, 2)
            dve.wait_ge(s_iota, 1)
            dve.wait_ge(s_edges, 16 * 8)

            for o, (key, other) in enumerate(((keys_i[1], keys_i[0]), (keys_i[0], keys_i[1]))):
                if o:
                    dve.wait_ge(s_stage, 2 * STEPS)
                V.tensor_copy(srec[:, :, 0], other)
                V.tensor_copy(srec[:, :, 2], weight[o])
                if not o:
                    V.tensor_scalar(srec[:, :, 3], place_i, E - 1, None, ALU.min)
                link(V.tensor_scalar(work_i, key, P - 1, None, ALU.bitwise_and))
                link(V.tensor_copy(low_f, work_i))
                V.tensor_copy(srec[:, :, 1], low_f)
                link(V.tensor_scalar(work_i, key, 7, None, ALU.logical_shift_right))
                V.tensor_copy(high_b, work_i)
                link(V.tensor_copy(high_f, work_i))

                with dve.Fori(0, STEPS) as i:
                    link.enter(i, 2 if o else 0)
                    for h in range(2):
                        c = bass.ds(i * (2 * GROUP) + h * GROUP, GROUP)
                        dve.wait_ge(s_ohused, i * 2 + (2 * STEPS * o + h + 1))
                        V.tensor_tensor(oh_low[h].rearrange("p (c n) -> p c n", n=P),
                                        iota_f[:].unsqueeze(1).to_broadcast([P, GROUP, P]),
                                        low_f[:, c].unsqueeze(2).to_broadcast([P, GROUP, P]), ALU.is_equal)
                        high = oh_high[h].rearrange("p (c n) -> p c n", n=NB)
                        ins = V.tensor_tensor(high, iota_f[:, 0:NB].unsqueeze(1).to_broadcast([P, GROUP, NB]),
                                              high_f[:, c].unsqueeze(2).to_broadcast([P, GROUP, NB]), ALU.is_equal)
                        if o:
                            link(ins)
                            ins = V.tensor_tensor(high, high, weight[1][:, c].unsqueeze(2).to_broadcast([P, GROUP, NB]), ALU.mult)
                        ins.then_inc(s_oh, 1)
                    link.leave(STEPS)
                dve.wait_ge(s_deg, o + 1)
                link(V.tensor_scalar((dis, diw)[o][:], bank[0][:, 0:NB], 1.0, None, ALU.add))

                with dve.Fori(0, BI) as i:
                    link.enter(i, 2)
                    for j in range(2):
                        b = bass.ds(i * 2 + j, 1)
                        link(V.tensor_scalar(masks[j], high_b, iota_f[:, b], None, ALU.is_equal, ALU.add, accum_out=cnt[:, b]))
                    link.leave(BI)
                V.memset(place, 0.0).then_inc(s_cnt, 1)

                dve.wait_ge(s_off, o + 1)
                first, tiles, ends, whole, start = small
                link(V.tensor_scalar(whole.bitcast(I32), bank[2][:, NB:2 * NB], P - 1.0, None, ALU.add))
                link(V.tensor_scalar(whole.bitcast(I32), whole.bitcast(I32), 7, None, ALU.logical_shift_right))
                link(V.tensor_copy(tiles, whole.bitcast(I32)))
                link(V.tensor_tensor_scan(ends, tiles, zero[:, 0:NB], 0.0, ALU.add, ALU.add))
                link(V.tensor_tensor(first, ends, tiles, ALU.subtract))
                link(V.scalar_tensor_tensor(start, first, float(P), bank[2][:, 0:NB], ALU.mult, ALU.add))
                link(V.tensor_tensor(blk_cmp.rearrange("p (t b) -> p t b", b=NB)[:, :, 0:NB - 1],
                                     tile_no.unsqueeze(2).to_broadcast([P, TW, NB - 1]),
                                     ends[:, 0:NB - 1].unsqueeze(1).to_broadcast([P, TW, NB - 1]), ALU.is_ge))
                link(V.tensor_reduce(blk_f, blk_cmp.rearrange("p (t b) -> p t b", b=NB)[:, :, 0:NB - 1], AX_X, ALU.add))
                V.tensor_scalar(blk_i[o], blk_f, float(D), None, ALU.mult).then_inc(s_blk, 1)

                with dve.Fori(0, BI) as i:
                    link.enter(i, 4)
                    for j in range(2):
                        V_ = V.tensor_scalar(masks[j], high_b, iota_f[:, bass.ds(i * 2 + j, 1)], None, ALU.is_equal)
                    link(V_)
                    for j in range(2):
                        V_ = V.tensor_tensor_scan(scans[j], masks[j], masks[j], start[:, bass.ds(i * 2 + j, 1)], ALU.add, ALU.max)
                    link(V_)
                    link(V.copy_predicated(place, masks[0].bitcast(U16), scans[0]))
                    link(V.copy_predicated(place, masks[1].bitcast(U16), scans[1]))
                    link.leave(BI)
                link(V.tensor_scalar(work_i, place, -1.0, None, ALU.add))
                link(V.tensor_scalar(place_i, work_i, P - 1, None, ALU.bitwise_and))
                link(V.tensor_scalar(work_i, work_i, 7, None, ALU.logical_shift_right))
                V.scalar_tensor_tensor(place_i, place_i, float(T), work_i, ALU.mult, ALU.add).then_inc(s_place, 1)

            V.memset(x_all[:, (N // P) * D:], 0.0)
            dve.wait_ge(s_place, 2)
            dve.wait_ge(s_blkst, 32)
            V.memset(fin[:], 0.0).then_inc(s_xfree, 1)

            roots = [0]

            def inverse_root(asked, w, to):
                roots[0] += 1
                asked.then_inc(s_root_in, 1)
                dve.wait_ge(s_root_out, roots[0])
                v, r, t = root_v[:, 0:w], root_r[:, 0:w], root_t[:, 0:w]
                link(V.reciprocal(r, r))
                link(V.tensor_tensor(t, v, r, ALU.mult))
                link(V.tensor_tensor(t, t, r, ALU.mult))
                link(V.tensor_scalar(t, t, -0.5, 1.5, ALU.mult, ALU.add))
                link(V.tensor_tensor(to, r, t, ALU.mult))

            dve.wait_ge(s_params, 16 * 28)
            inverse_root(V.tensor_copy(root_v[:, 0:NB], dis[:]), NB, dis[:])
            link(V.tensor_tensor(sq[:], root_v[:, 0:NB], dis[:], ALU.mult))
            link(V.tensor_scalar(tmpa[:], diw[:], 0.0, None, ALU.is_gt))
            inverse_root(V.tensor_scalar(root_v[:, 0:NB], diw[:], 1e-30, None, ALU.max), NB, diw[:])
            link(V.tensor_tensor(diw[:], diw[:], tmpa[:], ALU.mult))
            inverse_root(V.tensor_scalar(root_v[:, 0:KC], cols["var1"][:], EPS, None, ALU.add), KC, cols["var1"][:])
            link(V.tensor_tensor(cols["g1"][:], cols["g1"][:], cols["var1"][:], ALU.mult))
            link(V.tensor_tensor(cols["mu1"][:], cols["mu1"][:], cols["g1"][:], ALU.mult))
            link(V.tensor_tensor(cols["be1"][:], cols["be1"][:], cols["mu1"][:], ALU.subtract))
            inverse_root(V.tensor_scalar(root_v, rows["var2"][:], EPS, None, ALU.add), D, rows["var2"][:])
            link(V.tensor_tensor(rows["g2"][:], rows["g2"][:], rows["var2"][:], ALU.mult))
            link(V.tensor_tensor(rows["L2b2"][:], rows["L2b2"][:], rows["mu2"][:], ALU.subtract))
            link(V.tensor_tensor(rows["L2b2"][:], rows["L2b2"][:], rows["g2"][:], ALU.mult))
            link(V.tensor_tensor(rows["be2"][:], rows["be2"][:], rows["L2b2"][:], ALU.add))
            link(V.tensor_tensor(rows["L0a"][:], rows["L0a"][:], rows["L0r"][:], ALU.add))
            link(V.tensor_tensor(rows["L0b"][:], rows["L0b"][:], rows["L0r"][:], ALU.add))
            dve.wait_ge(s_nodes, 32 if N % P else 16)

            def statistics():
                with dve.Fori(0, BI) as i:
                    for j in range(2):
                        b = i * 2 + j
                        V.bn_stats(stats[:, bass.ds(b * 6, 6)], blk(x_all, b))
                st = stats[:].rearrange("p (b s) -> p b s", s=6)
                link(V.memset(tmpb[:], 0.0))
                link(V.tensor_tensor(tmpa[:], st[:, :, 1], st[:, :, 4], ALU.add))
                link(V.tensor_scalar(mean[:], tmpa[:], 0.5, None, ALU.mult))
                link(V.tensor_tensor(tmpa[:], st[:, :, 1], st[:, :, 4], ALU.subtract))
                link(V.scalar_tensor_tensor(tmpa[:], tmpa[:], 0.25, tmpa[:], ALU.mult, ALU.mult))
                link(V.tensor_tensor(tmpb[:], st[:, :, 2], st[:, :, 5], ALU.add))
                link(V.scalar_tensor_tensor(tmpa[:], tmpb[:], 1.0 / D, tmpa[:], ALU.mult, ALU.add))
                inverse_root(V.tensor_scalar(root_v[:, 0:NB], tmpa[:], EPS, None, ALU.add), NB, rstd[:])

            def norm(made):
                statistics()
                with dve.Fori(0, BI) as i:
                    for j in range(2):
                        b = i * 2 + j
                        dve.wait_ge(s_row, i * 2 + (NB * made + j + 1))
                        V.tensor_scalar(opa[:, j, :], blk(x_all, b), mean[:, bass.ds(b, 1)], rstd[:, bass.ds(b, 1)],
                                        ALU.subtract, ALU.mult).then_inc(s_z, 1)

            def edge_pass(m):
                o, weighted, attrs = PASSES[m]
                dve.wait_ge(s_recld, 32 * [1, 1, 2, 3, 3, 3][m])
                dve.wait_ge(s_tabst, 16 * (m + 1))
                with dve.Fori(0, ITER) as i:
                    for h in range(2):
                        dve.wait_ge(s_staged, i * 2 + (2 * ITER * m + h + 1))
                        for u in range(HALF):
                            k = h * HALF + u
                            dve.wait_ge(s_tile, i * RING + (T * m + k + 1))
                            place_, w = low[:, h, 2 * u:2 * u + 1], low[:, h, 2 * u + 1:2 * u + 2]
                            if weighted:
                                ins = V.tensor_scalar(onehot[:, k, :], iota_f[:], place_, w, ALU.is_equal, ALU.mult)
                            else:
                                ins = V.tensor_scalar(onehot[:, k, :], iota_f[:], place_, None, ALU.is_equal)
                            ins.then_inc(s_onehot, 1)
                        if attrs:
                            for u in range(HALF):
                                k = h * HALF + u
                                dve.wait_ge(s_gath[k], i * 16 + 16 * (ITER * m + 1))
                                dve.wait_ge(s_egath[k], i * 16 + 16)
                                V.tensor_tensor(gbuf[:, k, :], gbuf[:, k, :], ebuf[:, k, :], ALU.add).then_inc(s_msg, 1)
                        for u in range(HALF):
                            k = h * HALF + u
                            r = dve.value_load(row0[0:1, bass.ds(i * RING + k, 1)], min_val=0, max_val=(NB - 1) * D)
                            to = acc[:, bass.ds(r, D)]
                            dve.wait_ge(s_tile, i * RING + (T * m + k + 1 + RING))
                            dve.wait_ge(s_added, i * RING + (T * m + k + BANKS))
                            V.tensor_tensor(to, to, bank[k % BANKS][:, 0:D], ALU.add).then_inc(s_added, 1)

            def dense(q):
                kind = DENSE[q]
                n = NB * q
                dve.wait_ge(s_added, T * {"gcn0": 1, "gcn1": 2, "mlp": 3, "gine": 4, "lin1": 4, "lin2": 5, "last": 6}[kind] + BANKS)
                dve.wait_ge(s_done, n + 2)
                row = {"gcn0": "L0a", "gcn1": "L0b", "mlp": "L1b2", "lin1": "L3b1", "lin2": "L3b2"}.get(kind)
                with dve.Fori(0, BI) as i:
                    steps = {"gcn0": 1, "gcn1": 1, "mlp": 1, "gine": 3, "lin1": 1, "lin2": 1, "last": 1}[kind]
                    link.enter(i, steps)
                    bs = [i * 2, i * 2 + 1]
                    col = [bass.ds(b, 1) for b in bs]
                    if kind != "last":
                        for j in range(2):
                            a = blk(acc, bs[j])
                            dve.wait_ge(s_done, i * 2 + (n + j + 1))
                            if kind in READS_TABLE:
                                dve.wait_ge(s_tin[j], i * 16 + 16 * (BI * READS_TABLE.index(kind) + 1))
                            if kind in ("gcn0", "gcn1"):
                                V.tensor_scalar(opa[:, j, :], a, dis[:, col[j]], None, ALU.mult)
                                ins = V.tensor_scalar(opb[:, j, :], tin[:, j, :], sq[:, col[j]], None, ALU.mult)
                            elif kind == "mlp":
                                ins = V.tensor_scalar(opa[:, j, :], a, diw[:, col[j]], None, ALU.mult)
                            elif kind == "gine":
                                ins = V.tensor_tensor(opa[:, j, :], a, tin[:, j, :], ALU.add)
                            elif kind == "lin1":
                                ins = V.tensor_scalar(opa[:, j, :], blk(x_all, bs[j]), mean[:, col[j]], rstd[:, col[j]],
                                                      ALU.subtract, ALU.mult)
                            else:
                                ins = V.tensor_scalar(opa[:, j, :], a, dis[:, col[j]], 0.0, ALU.mult, ALU.max)
                            ins.then_inc(s_op, 1)

                    def first(j):
                        if kind == "last":
                            dve.wait_ge(s_done, i * 2 + (n + j + 1))
                            return V.tensor_scalar(fin[:, j, :], blk(acc, bs[j]), dis[:, col[j]], 0.0, ALU.mult, ALU.max)
                        dve.wait_ge(s_pf, i * 2 + (n + j + 1))
                        return V.tensor_tensor(fin[:, j, :], bank[j][:, 0:D], opa[:, j, :] if kind == "gine" else rows[row][:], ALU.add)

                    first(0)
                    link(first(1))
                    if kind == "gine":
                        for op, r in ((ALU.mult, "g2"), (ALU.add, "be2")):
                            V.tensor_tensor(fin[:, 0, :], fin[:, 0, :], rows[r][:], op)
                            link(V.tensor_tensor(fin[:, 1, :], fin[:, 1, :], rows[r][:], op))
                    for j in range(2):
                        xb, ab = blk(x_all, bs[j]), blk(acc, bs[j])
                        if kind == "gcn0":
                            ins = V.tensor_scalar(ab, fin[:, j, :], dis[:, col[j]], 0.0, ALU.mult, ALU.max)
                        elif kind in ("lin1", "lin2"):
                            ins = V.tensor_scalar(ab, fin[:, j, :], dis[:, col[j]], None, ALU.mult)
                        elif kind == "gcn1":
                            ins = V.scalar_tensor_tensor(xb, fin[:, j, :], 0.0, xb, ALU.max, ALU.add)
                        else:
                            ins = V.tensor_tensor(xb, xb, fin[:, j, :], ALU.add)
                        ins.then_inc(s_done, 1)
                    link.leave(BI)
                dve.wait_ge(s_done, n + NB + 2)

            norm(0)
            edge_pass(0)
            dense(0)
            edge_pass(1)
            dense(1)
            norm(1)
            edge_pass(2)
            dense(2)
            norm(2)
            edge_pass(3)
            dense(3)
            statistics()
            dense(4)
            edge_pass(4)
            dense(5)
            edge_pass(5)
            dense(6)


_INS = ["x", "src", "dst", "edge_attr_256", "edge_weight", "edge_weight1",
        "L0_gnn_W", "L0_gnn_b", "L0_gnn_resW", "L0_gnn_resb",
        "L1_gnn_W", "L1_gnn_b", "L1_gnn_W1", "L1_gnn_b1", "L1_gnn_W2", "L1_gnn_b2",
        "L2_gnn_W1", "L2_gnn_b1", "L2_gnn_W2", "L2_gnn_b2",
        "L2_gnn_bn1_gamma", "L2_gnn_bn1_beta", "L2_gnn_bn1_mean", "L2_gnn_bn1_var",
        "L2_gnn_bn2_gamma", "L2_gnn_bn2_beta", "L2_gnn_bn2_mean", "L2_gnn_bn2_var",
        "L3_gnn_W1", "L3_gnn_b1", "L3_gnn_W2", "L3_gnn_b2"]
_TURNED = ("L2_gnn_W1", "L2_gnn_W2", "L3_gnn_W1", "L3_gnn_W2")


def kernel(**inputs):
    import numpy as np
    import concourse.bacc as bacc
    from concourse.bass_utils import run_bass_kernel_spmd

    nc = bacc.Bacc("TRN2", target_bir_lowering=False, num_devices=1)
    arrays, io = {}, {}
    for name in _INS:
        a = np.asarray(inputs[name])
        a = np.ascontiguousarray(a.T if name in _TURNED else a)
        arrays[f"in_{name}"] = a
        io[name] = nc.dram_tensor(f"in_{name}", a.shape, mybir.dt.from_np(a.dtype), kind="ExternalInput").ap()
    out = nc.dram_tensor("out_0", io["x"].shape, F32, kind="ExternalOutput").ap()
    build(nc, io, out)
    r = run_bass_kernel_spmd(nc, [arrays], core_ids=[0])
    return r.results[0]["out_0"]
```

```python
from contextlib import ExitStack

import concourse.bass as bass
from concourse import mybir

P = 128
F32 = mybir.dt.float32
BF16 = mybir.dt.bfloat16
I32 = mybir.dt.int32
U16 = mybir.dt.uint16
ALU = mybir.AluOpType
ACT = mybir.ActivationFunctionType
AX_X = mybir.AxisListType.X
EPS = 1e-5

HALF = 8
RING = 2 * HALF
LAG = 4
BANKS = 4
LOADS = 4


class Chain:

    def __init__(self, eng, sem):
        self.eng, self.sem, self.n, self.i, self.per = eng, sem, 0, None, 0

    def __call__(self, ins):
        self.n += 1
        ins.then_inc(self.sem, 1)
        self.eng.wait_ge(self.sem, self.n if self.i is None else self.i * self.per + self.n)
        if self.i is not None:
            self.eng.nop(nofuse=True)

    def enter(self, i, per):
        self.i, self.per, self.start = i, per, self.n

    def leave(self, iterations):
        assert self.n - self.start == self.per
        self.n += self.per * (iterations - 1)
        self.i = None


def build(nc, io, out):
    N, D = io["x"].shape
    E = io["src"].shape[0]
    KC = D // P
    NB = -(-N // P)
    NB += NB % 2
    if NB * P == N:
        NB += 2
    COLS = -(-E // P)
    PAD_NODE = (NB - 1) * P
    T = (COLS * P + NB * (P - 1)) // P
    T = -(-T // RING) * RING
    GROUP = next(g for g in range(20, 0, -1) if COLS % (2 * g) == 0)
    STEPS = COLS // (2 * GROUP)
    TW = -(-T // P)
    FIELDS = 4
    LAST = E - (P - 1) * COLS
    assert (NB - 1) * P >= N and 0 < LAST <= COLS and D == KC * P

    with ExitStack() as ctx:
        def sb(name, shape, dt=F32):
            return ctx.enter_context(nc.sbuf_tensor(name, shape, dt))

        def sem(name):
            return ctx.enter_context(nc.semaphore(name))

        table = nc.dram_tensor("table", (NB * P, D), F32, kind="Internal").ap()
        records = [nc.dram_tensor(f"records{o}", (P * T, FIELDS), F32, kind="Internal").ap() for o in range(2)]
        blockrow = [nc.dram_tensor(f"blockrow{o}", (P * TW,), I32, kind="Internal").ap() for o in range(2)]
        startrow = nc.dram_tensor("startrow", (P * TW,), I32, kind="Internal").ap()
        chunks = [nc.dram_tensor(f"chunks{f}", (COLS, P), (I32, I32, F32)[f], kind="Internal").ap() for f in range(3)]

        x_all = sb("x_all", [P, NB * D])
        acc = sb("acc", [P, NB * D])
        rec = sb("rec", [P, T * FIELDS])
        row0 = sb("row0", [1, T], I32)
        first_edge = sb("first_edge", [1, T], I32)
        unsorted = sb("unsorted", [P, 1], I32)
        gbuf = sb("gbuf", [P, RING, D])
        ebuf = sb("ebuf", [P, RING, D])
        onehot = sb("onehot", [P, RING, P])
        idx = sb("idx", [P, 2, HALF], I32)
        eidx = sb("eidx", [P, 2, HALF], I32)
        low = sb("low", [P, 2, HALF * 2])

        iota_f = sb("iota_f", [P, P])
        iota_b = sb("iota_b", [P, P], BF16)
        ident = sb("ident", [P, P])
        tri = sb("tri", [P, P])
        ones = sb("ones", [P, P])
        zero = sb("zero", [P, P])
        w_late = sb("w_late", [P, 7, KC, D])
        W = {k: sb("w_" + k, [P, KC, D])[:] for k in ("L0a", "L0b", "L0r")}
        W.update({k: w_late[:, n] for n, k in enumerate(("L1", "L1a", "L1b", "L2a", "L2b", "L3a", "L3b"))})
        rows = {k: sb("row_" + k, [P, D]) for k in
                ("L0a", "L0b", "L1b2", "L3b1", "L3b2", "g2", "be2")}
        cols = {k: sb("col_" + k, [P, KC]) for k in ("L1b", "L1b1", "L2b1", "g1", "be1", "mu1", "var1")}
        stats = sb("stats", [P, NB * 6])
        mean, rstd = sb("mean", [P, NB]), sb("rstd", [P, NB])
        tmpa, tmpb = sb("tmpa", [P, NB]), sb("tmpb", [P, NB])
        dis, sq, diw = sb("dis", [P, NB]), sb("sq", [P, NB]), sb("diw", [P, NB])

        tin = sb("tin", [P, 2, D])
        opa, opb = sb("opa", [P, 2, D]), sb("opb", [P, 2, D])
        opT = sb("opT", [P, 2, 2 * D])
        root_v, root_r, root_t = opT[:, 0, 0:D], opT[:, 0, D:2 * D], opT[:, 1, 0:D]
        mid1, mid2 = opb, tin
        fin = sb("fin", [P, 2, D])
        rows.update({"L0r": opb[:, 0, :], "mu2": opb[:, 1, :], "var2": tin[:, 0, :], "L2b2": tin[:, 1, :]})

        class Lent:

            def __init__(self, t):
                self.t, self.at = t, 0

            def __call__(self, words, dt=F32):
                a = self.t[:, self.at:self.at + words]
                self.at += words
                assert self.at <= self.t.shape[1]
                return a if dt == F32 else a.bitcast(dt)

        HW = -(-COLS // 2)
        lend = Lent(acc[:])
        src_i, dst_i, dst_next = (lend(COLS, I32) for _ in range(3))
        weight1, edge_no = lend(COLS), lend(COLS, I32)
        low_f, high_f, high_b = lend(COLS), lend(COLS), lend(HW, BF16)[:, 0:COLS]
        work_i, place, place_i = lend(COLS, I32), lend(COLS), lend(COLS, I32)
        mask = lend(HW, BF16)[:, 0:COLS]
        begun, step_f, hit = lend(COLS), lend(COLS), lend(COLS)
        lend = Lent(x_all[:])
        oh_low = [lend(GROUP * P) for _ in range(2)]
        oh_high = [lend(GROUP * NB) for _ in range(2)]
        blk_cmp, blk_f = lend(TW * NB), lend(TW)
        run_i = [lend(TW * P, I32), lend(TW * P, I32), lend(TW * P)]
        run_f = [lend(TW * P) for _ in range(2)]
        edge_ends = lend(2 * COLS, I32)[0:1, :]
        PADS = COLS * P - E
        pads = [lend(PADS, (I32, I32, F32)[f])[0:1, :] for f in range(3)]
        lend = Lent(ebuf[:].rearrange("p r d -> p (r d)"))
        dst1_i, low1, weight, place1_i = lend(COLS, I32), lend(COLS), lend(COLS), lend(COLS, I32)
        high1_b = lend(HW, BF16)[:, 0:COLS]
        lend = Lent(w_late[:].rearrange("p a k d -> p (a k d)"))
        place1, scan1 = lend(COLS), lend(COLS)
        spare = lend(COLS)
        mask1 = lend(HW, BF16)[:, 0:COLS]
        flat = w_late[:].rearrange("p a k d -> p (a k d)")
        oh1_low = flat[:, 0:GROUP * P]
        oh1_high = flat[:, 3 * COLS:3 * COLS + GROUP * NB]
        scan = onehot[:].rearrange("p r n -> p (r n)")[:, 0:COLS]
        small = sb("small", [P, 8 * NB])
        cnt, first, tiles, ends, whole = (small[:, k * NB:(k + 1) * NB] for k in range(5))
        start = [small[:, (5 + o) * NB:(6 + o) * NB] for o in range(2)]
        tabs = sb("tabs", [P, 8 * TW])
        tile_no, t_chunk, t_block, t_base = (tabs[:, k * TW:(k + 1) * TW] for k in range(4))
        blk_i = [tabs[:, (4 + o) * TW:(5 + o) * TW].bitcast(I32) for o in range(2)]
        chunk_i, first_i = (tabs[:, k * TW:(k + 1) * TW].bitcast(I32) for k in (6, 7))
        stage_idx = sb("stage_idx", [P, 2, GROUP], I32)
        stage_rec = sb("stage_rec", [P, 2, GROUP * FIELDS])

        bank = [ctx.enter_context(nc.psum_tensor(f"bank{k}", [P, 512], F32)) for k in range(8)]

        TURN = (4, 5, 6, 7, 1, 3)

        s_pads, s_iota, s_unfilled, s_xfree = (sem(k) for k in ("pads_written", "constants_ready", "unfilled_ready", "x_free"))
        s_edges, s_ends, s_chunks = sem("edges_loaded"), sem("run_ends_loaded"), sem("runs_laid_out")
        s_nodes, s_params, s_late = sem("nodes_loaded"), sem("params_loaded"), sem("late_weights_loaded")
        s_chain, s_pchain = sem("vector_chain"), sem("pool_chain")
        s_gchain, s_schain = sem("vector_chain_general"), sem("vector_chain_sorted")
        s_spchain = [sem(f"pool_staged_order{o}") for o in range(2)]
        s_root_in, s_root_out = sem("root_asked"), sem("root_taken")
        s_viol, s_violsum, s_flag = sem("inversions_ready"), sem("inversions_summed"), sem("unsorted_known")
        s_rows, s_rowsout = sem("run_tables_ready"), sem("run_tables_spread")
        s_tiles, s_runs, s_lows = sem("tile_tables_ready"), sem("runs_gathered"), sem("run_places_ready")
        s_runT, s_built, s_recst = sem("runs_turned"), sem("records_built"), sem("records_stored")
        s_oh, s_ohused = ([sem(f"degree_onehots_{k}{o}") for o in range(2)] for k in ("ready", "used"))
        s_deg = [sem(f"degrees_ready{o}") for o in range(2)]
        s_cnt, s_off = ([sem(f"{k}_ready{o}") for o in range(2)] for k in ("counts", "offsets"))
        s_prefill, s_place = sem("records_prefilled"), [sem(f"places_ready{o}") for o in range(2)]
        s_blk, s_blkst = ([sem(f"blocks_{k}{o}") for o in range(2)] for k in ("ready", "stored"))
        s_scat = [[sem(f"scattered{o}{h}") for h in range(2)] for o in range(2)]
        s_recld = sem("records_loaded")
        s_staged = sem("indices_staged")
        s_gath = [sem(f"gathered{k}") for k in range(RING)]
        s_egath = [sem(f"edges_gathered{k}") for k in range(RING)]
        s_msg, s_relu = sem("messages_added"), sem("messages_ready")
        s_onehot, s_tile, s_added = sem("onehot_ready"), sem("tile_summed"), sem("tile_added")
        s_z, s_row = sem("normalized"), sem("table_rows_ready")
        s_tabst = sem("table_stored")
        s_tin = [sem(f"table_block{k}_loaded") for k in range(2)]
        s_op, s_turn, s_turned = sem("operands_ready"), sem("operands_turned"), sem("turned_copied")
        s_m1, s_m1o = sem("first_product"), sem("first_copied")
        s_m2, s_m2o = sem("second_product"), sem("second_copied")
        s_pf, s_done = sem("last_product"), sem("block_done")
        s_out = sem("output_stored")

        PASSES = [(0, False, False), (0, False, False), (1, True, False),
                  (0, False, True), (0, True, False), (0, True, False)]
        DENSE = ["gcn0", "gcn1", "mlp", "gine", "lin1", "lin2", "last"]
        READS_TABLE = ["gcn0", "gcn1", "gine"]
        FIRST_MID = ["mlp", "gine"]
        ITER = T // RING
        BI = NB // 2
        PART = 9
        PARAMS = 3 + 11 + 7
        EXTRA = {0: NB, 1: 2 * STEPS}
        assert max(EXTRA.values()) < ITER and 0 < PART < STEPS

        def blk(t, b):
            return t[:, bass.ds(b * D, D)]

        def load_row(t, at, engine, most):
            return nc.values_load_multi_w_load_instructions(
                t[0:1, bass.ds(at, LOADS)], engines=(engine,), min_val=0, max_val=most,
                skip_runtime_bounds_check_because="VectorE has cut the values to their range")[1]

        block = ctx.enter_context(nc.Block())

        @block.sync
        def _(sp):
            sp.wait_ge(s_pads, 1)
            ew1 = io["edge_weight1"].rearrange("e a -> (e a)")
            for to, a, n in ((dst_i, io["dst"], E), (dst_next, io["dst"][1:E], E - 1), (src_i, io["src"], E), (weight1, ew1, E),
                             (weight, io["edge_weight"], E), (dst1_i, io["dst"], E)):
                sp.dma_start(to[0:P - 1, :], a[0:(P - 1) * COLS].rearrange("(p c) -> p c", c=COLS)).then_inc(s_edges, 16)
                left = n - (P - 1) * COLS
                sp.dma_start(to[P - 1:P, 0:left], a[(P - 1) * COLS:n].rearrange("(p c) -> p c", p=1)).then_inc(s_edges, 16)
            whole_runs = (COLS - 1) * P
            with nc.allow_non_contiguous_dma(reason="one element of each run of 128 edges"):
                for k, at in enumerate((0, P - 1)):
                    sp.dma_start(edge_ends[:, k * COLS:(k + 1) * COLS - 1],
                                 io["dst"][0:whole_runs].rearrange("(a c e) -> a c e", e=P, a=1)[:, :, at]).then_inc(s_ends, 16)
                for k, at in enumerate((whole_runs, E - 1)):
                    sp.dma_start(edge_ends[:, (k + 1) * COLS - 1:(k + 1) * COLS],
                                 io["dst"][at:at + 1].rearrange("(a c) -> a c", a=1)).then_inc(s_ends, 16)
            for f, a in enumerate((io["src"], io["dst"], ew1)):
                sp.dma_start(chunks[f][0:COLS - 1], a[0:whole_runs].rearrange("(c e) -> c e", e=P)).then_inc(s_chunks, 16)
                sp.dma_start(chunks[f][COLS - 1:COLS, 0:PADS], pads[f]).then_inc(s_chunks, 16)
                sp.dma_start(chunks[f][COLS - 1:COLS, PADS:P], a[whole_runs:E].rearrange("(c e) -> c e", c=1)).then_inc(s_chunks, 16)
            sp.wait_ge(s_unfilled, 1)
            for o in range(2):
                sp.dma_start(records[o].rearrange("(p t) f -> p (t f)", p=P), rec[:]).then_inc(s_prefill, 16)
            for k, a in (("L0a", io["L0_gnn_W"][0]), ("L0b", io["L0_gnn_W"][1]), ("L0r", io["L0_gnn_resW"])):
                sp.dma_start(W[k], a.rearrange("(k p) n -> p k n", p=P)).then_inc(s_params, 16)
            for k, a in (("L0a", io["L0_gnn_b"][0]), ("L0b", io["L0_gnn_b"][1]), ("L0r", io["L0_gnn_resb"]),
                         ("L1b2", io["L1_gnn_b2"]), ("L3b1", io["L3_gnn_b1"]), ("L3b2", io["L3_gnn_b2"]),
                         ("g2", io["L2_gnn_bn2_gamma"]), ("be2", io["L2_gnn_bn2_beta"]), ("mu2", io["L2_gnn_bn2_mean"]),
                         ("var2", io["L2_gnn_bn2_var"]), ("L2b2", io["L2_gnn_b2"])):
                sp.dma_start(rows[k][:], a.partition_broadcast(P)).then_inc(s_params, 16)
            with nc.allow_non_contiguous_dma(reason="seven vectors of 256, one element per partition"):
                for k, a in (("L1b", io["L1_gnn_b"]), ("L1b1", io["L1_gnn_b1"]), ("L2b1", io["L2_gnn_b1"]),
                             ("g1", io["L2_gnn_bn1_gamma"]), ("be1", io["L2_gnn_bn1_beta"]),
                             ("mu1", io["L2_gnn_bn1_mean"]), ("var1", io["L2_gnn_bn1_var"])):
                    sp.dma_start(cols[k][:], a.rearrange("(m p) -> p m", p=P)).then_inc(s_params, 16)

            def by_tile(dram):
                return dram.rearrange("(j p) -> p j", p=P)

            def as_row(dram):
                return dram[0:T].rearrange("(a t) -> a t", a=1)

            with nc.allow_non_contiguous_dma(reason="seven words per partition, in tiles' order"):
                sp.wait_ge(s_blk[1], 1)
                sp.dma_start(by_tile(blockrow[1]), blk_i[1]).then_inc(s_blkst[1], 16)
                sp.wait_ge(s_flag, 1)
                mixed = sp.value_load(unsorted[0:1, 0:1], min_val=0, max_val=1)
                with sp.If(mixed > 0):
                    sp.wait_ge(s_ends, 64)
                    sp.wait_ge(s_chunks, 16 * 9)
                    sp.wait_ge(s_blk[0], 1)
                    sp.dma_start(by_tile(blockrow[0]), blk_i[0]).then_inc(s_blkst[0], 16)
                    sp.wait_ge(s_blkst[0], 16)
                    for h in range(2):
                        sp.wait_ge(s_scat[0][h], 16 * GROUP * STEPS)
                    sp.dma_start(rec[:], records[0].rearrange("(p t) f -> p (t f)", p=P)).then_inc(s_recld, 16)
                    sp.dma_start(row0[:], as_row(blockrow[0])).then_inc(s_recld, 16)
                with sp.Else():
                    sp.wait_ge(s_tiles, 1)
                    sp.dma_start(by_tile(blockrow[0]), blk_i[0]).then_inc(s_blkst[0], 16)
                    sp.dma_start(by_tile(startrow), first_i).then_inc(s_blkst[0], 16)
                    sp.wait_ge(s_blkst[0], 32)
                    sp.dma_start(first_edge[:], as_row(startrow)).then_inc(s_recld, 16)
                    sp.wait_ge(s_built, 1)
                    sp.dma_start(records[0].rearrange("(p t) f -> p (t f)", p=P), rec[:]).then_inc(s_recst, 16)
                    sp.dma_start(row0[:], as_row(blockrow[0])).then_inc(s_recld, 16)
                    sp.wait_ge(s_recst, 16)
            sp.wait_ge(s_xfree, 1)
            full = N // P
            sp.dma_start(x_all[:, 0:full * D].rearrange("p (b d) -> p b d", d=D),
                         io["x"][0:full * P].rearrange("(b p) d -> p b d", p=P)).then_inc(s_nodes, 16)
            if N % P:
                sp.dma_start(x_all[0:N % P, full * D:(full + 1) * D], io["x"][full * P:N]).then_inc(s_nodes, 16)

            table_b = table.rearrange("(b p) d -> p b d", p=P)

            def load_records(o):
                sp.dma_start(rec[:], records[o].rearrange("(p t) f -> p (t f)", p=P)).then_inc(s_recld, 16)
                sp.dma_start(row0[:], as_row(blockrow[o])).then_inc(s_recld, 16)

            def store_table(made, before):
                sp.wait_ge(made, before + NB)
                sp.dma_start(table_b, acc[:].rearrange("p (b d) -> p b d", d=D)).then_inc(s_tabst, 16)

            def load_edges(m):
                with sp.Fori(0, ITER) as i:
                    for k in range(RING):
                        if k % LOADS == 0:
                            starts = load_row(first_edge, i * RING + k, mybir.EngineType.SP, E - P)
                        e = starts[k % LOADS]
                        sp.wait_ge(s_tile, i * RING + (T * m + k + 1))
                        sp.nop(nofuse=True)
                        sp.dma_start(ebuf[:, k, :], io["edge_attr_256"][bass.ds(e, P), :]).then_inc(s_egath[k], 16)

            def read_table(q):
                r = READS_TABLE.index(DENSE[q])
                sp.wait_ge(s_tabst, 16 * (1 + [0, 1, 3][r]))
                with sp.Fori(0, BI) as i:
                    for j in range(2):
                        sp.wait_ge(s_op, i * 2 + (NB * q + j + 1))
                        sp.dma_start(tin[:, j, :], table_b[:, bass.ds(i * 2 + j, 1), :].rearrange("p b d -> p (b d)")
                                     ).then_inc(s_tin[j], 16)

            store_table(s_row, 2)
            read_table(0)
            store_table(s_done, 2)
            read_table(1)
            store_table(s_row, 2 + NB)
            for h in range(2):
                sp.wait_ge(s_scat[1][h], 16 * GROUP * STEPS)
            sp.wait_ge(s_blkst[1], 16)
            load_records(1)
            for k, a in (("L1", io["L1_gnn_W"]), ("L1a", io["L1_gnn_W1"]), ("L1b", io["L1_gnn_W2"]),
                         ("L2a", io["L2_gnn_W1"]), ("L2b", io["L2_gnn_W2"]),
                         ("L3a", io["L3_gnn_W1"]), ("L3b", io["L3_gnn_W2"])):
                sp.dma_start(W[k], a.rearrange("(k p) n -> p k n", p=P)).then_inc(s_late, 16)
            store_table(s_row, 2 + 2 * NB)
            load_records(0)
            mixed = sp.value_load(unsorted[0:1, 0:1], min_val=0, max_val=1)
            with sp.If(mixed < 1):
                load_edges(3)
            read_table(3)
            store_table(s_done, 2 + 4 * NB)
            store_table(s_done, 2 + 5 * NB)
            sp.wait_ge(s_done, 2 + 7 * NB)
            sp.dma_start(out[0:full * P].rearrange("(b p) d -> p b d", p=P),
                         x_all[:, 0:full * D].rearrange("p (b d) -> p b d", d=D)).then_inc(s_out, 16)
            if N % P:
                sp.dma_start(out[full * P:N], x_all[0:N % P, full * D:(full + 1) * D]).then_inc(s_out, 16)
            sp.wait_ge(s_out, 32 if N % P else 16)

        @block.gpsimd
        def _(pool):
            link = Chain(pool, s_pchain)
            nc.gpsimd.iota(iota_f[:], pattern=[[1, P]], base=0, channel_multiplier=0,
                           allow_small_or_imprecise_dtypes=True)
            nc.gpsimd.iota(tile_no, pattern=[[P, TW]], base=0, channel_multiplier=1,
                           allow_small_or_imprecise_dtypes=True)
            link(nc.gpsimd.memset(ident[:], 0.0))
            link(nc.gpsimd.affine_select(out=ident[:], in_=ident[:], compare_op=ALU.not_equal, fill=1.0, base=0,
                                         pattern=[[-1, P]], channel_multiplier=1))
            link(nc.gpsimd.memset(tri[:], 0.0))
            link(nc.gpsimd.affine_select(out=tri[:], in_=tri[:], compare_op=ALU.is_ge, fill=1.0, base=0,
                                         pattern=[[-1, P]], channel_multiplier=1))
            nc.gpsimd.iota(edge_no, pattern=[[1, COLS]], base=0, channel_multiplier=COLS).then_inc(s_iota, 1)

            def scatter(i, o, h, staged):
                at = bass.ds(i * (2 * GROUP) + h * GROUP, GROUP)
                to = stage_rec[:, h, :].rearrange("p (u f) -> p u f", f=FIELDS)
                fields = (src_i, low_f, weight1, edge_no) if o == 0 else (dst1_i, low1, weight)
                for f, a in enumerate(fields):
                    nc.gpsimd.tensor_copy(to[:, :, f], a[:, at])
                nc.gpsimd.tensor_copy(stage_idx[:, h, :], (place_i, place1_i)[o][:, at]).then_inc(s_spchain[o], 1)
                pool.wait_ge(s_spchain[o], staged)
                pool.nop(nofuse=True)
                for u in range(GROUP):
                    nc.gpsimd.indirect_dma_start(
                        out=records[o][:, :], out_offset=bass.IndirectOffsetOnAxis(ap=stage_idx[:, h, u:u + 1], axis=0),
                        in_=stage_rec[:, h, u * FIELDS:(u + 1) * FIELDS], in_offset=None).then_inc(s_scat[o][h], 16)

            def scatters(o, lo, hi):
                if lo == 0:
                    for h in range(2):
                        scatter(0, o, h, h + 1)
                    lo = 1
                with pool.Fori(lo, hi) as i:
                    for h in range(2):
                        pool.wait_ge(s_scat[o][h], i * (16 * GROUP))
                        pool.nop(nofuse=True)
                        scatter(i, o, h, i * 2 + (h + 1))

            link(nc.gpsimd.memset(stage_rec[:], 0.0))
            pool.wait_ge(s_flag, 1)
            mixed = pool.value_load(unsorted[0:1, 0:1], min_val=0, max_val=1)
            with pool.If(mixed > 0):
                pool.wait_ge(s_prefill, 32)
                pool.wait_ge(s_place[0], 1)
                scatters(0, 0, STEPS)
                for h in range(2):
                    pool.wait_ge(s_scat[0][h], 16 * GROUP * STEPS)
            with pool.Else():
                pool.wait_ge(s_chunks, 16 * 9)
                pool.wait_ge(s_tiles, 1)
                for f in range(3):
                    for j in range(TW):
                        nc.gpsimd.indirect_dma_start(
                            out=run_i[f][:, j * P:(j + 1) * P], out_offset=None, in_=chunks[f][:, :],
                            in_offset=bass.IndirectOffsetOnAxis(ap=chunk_i[:, j:j + 1], axis=0)).then_inc(s_runs, 16)

            def edge_pass(m, gather_edges):
                pool.wait_ge(s_tabst, 16 * (m + 1))
                with pool.Fori(0, ITER) as i:
                    for h in range(2):
                        pool.wait_ge(s_staged, i * 2 + (2 * ITER * m + h + 1))
                        pool.nop(nofuse=True)
                        for u in range(HALF):
                            k = h * HALF + u
                            nc.gpsimd.indirect_dma_start(
                                out=gbuf[:, k, :], out_offset=None, in_=table[:, :],
                                in_offset=bass.IndirectOffsetOnAxis(ap=idx[:, h, u:u + 1], axis=0)).then_inc(s_gath[k], 16)
                            if gather_edges:
                                nc.gpsimd.indirect_dma_start(
                                    out=ebuf[:, k, :], out_offset=None, in_=io["edge_attr_256"][:, :],
                                    in_offset=bass.IndirectOffsetOnAxis(ap=eidx[:, h, u:u + 1], axis=0)).then_inc(s_egath[k], 16)

            edge_pass(0, False)
            pool.wait_ge(s_prefill, 32)
            pool.wait_ge(s_place[1], 1)
            scatters(1, 0, PART)
            edge_pass(1, False)
            scatters(1, PART, STEPS)
            edge_pass(2, False)
            mixed = pool.value_load(unsorted[0:1, 0:1], min_val=0, max_val=1)
            with pool.If(mixed > 0):
                edge_pass(3, True)
            with pool.Else():
                edge_pass(3, False)
            edge_pass(4, False)
            edge_pass(5, False)

        @block.scalar
        def _(act):
            roots = [0]

            def root(v, r):
                roots[0] += 1
                act.wait_ge(s_root_in, roots[0])
                nc.scalar.activation(r, v, ACT.Sqrt).then_inc(s_root_out, 1)

            root(root_v[:, 0:NB], root_r[:, 0:NB])
            root(root_v[:, 0:KC], root_r[:, 0:KC])
            root(root_v, root_r)

            def edge_pass(m):
                o, weighted, attrs = PASSES[m]
                act.wait_ge(s_recld, 32 * [1, 1, 2, 3, 3, 3][m])
                recs = rec[:].rearrange("p (t f) -> p t f", f=FIELDS)

                def stage(i, h):
                    act.wait_ge(s_tile, i * RING + (T * m + HALF * (h + 1)))
                    act.nop(nofuse=True)
                    at = bass.ds(i * RING + h * HALF, HALF)
                    nc.scalar.copy(idx[:, h, :], recs[:, at, 0])
                    if attrs:
                        nc.scalar.copy(eidx[:, h, :], recs[:, at, 3])
                    nc.scalar.copy(low[:, h, :].rearrange("p (t f) -> p t f", f=2), recs[:, at, 1:3]).then_inc(s_staged, 1)

                def cut_messages(i, h):
                    for u in range(HALF):
                        k = h * HALF + u
                        act.wait_ge(s_msg, i * RING + (k + 1))
                        nc.scalar.activation(gbuf[:, k, :], gbuf[:, k, :], ACT.Relu).then_inc(s_relu, 1)

                if not attrs:
                    with act.Fori(0, ITER) as i:
                        for h in range(2):
                            stage(i, h)
                    return
                stage(0, 0)
                with act.Fori(0, ITER - 1) as i:
                    stage(i, 1)
                    cut_messages(i, 0)
                    stage(i + 1, 0)
                    cut_messages(i, 1)
                stage(ITER - 1, 1)
                cut_messages(ITER - 1, 0)
                cut_messages(ITER - 1, 1)

            def norm(scale, made):
                root(root_v[:, 0:NB], root_r[:, 0:NB])
                with act.Fori(0, BI) as i:
                    for j in range(2):
                        act.wait_ge(s_z, i * 2 + (NB * made + j + 1))
                        act.nop(nofuse=True)
                        b = i * 2 + j
                        nc.scalar.activation(blk(acc, b), opa[:, j, :], ACT.Relu,
                                             scale=1.0 if scale is None else scale[:, bass.ds(b, 1)]).then_inc(s_row, 1)

            def dense(q):
                kind = DENSE[q]
                if kind == "last":
                    return
                n = NB * q
                two = kind in ("gcn0", "gcn1")
                with act.Fori(0, BI) as i:
                    for j in range(2):
                        act.wait_ge(s_turn, i * 2 + (n + j + 1))
                        width = 2 * D if two else D
                        if kind == "gine":
                            for c in range(KC):
                                ins = nc.scalar.activation(opT[:, j, c * P:(c + 1) * P], bank[4 + j][:, c * P:(c + 1) * P], ACT.Identity,
                                                           bias=cols["be1"][:, c:c + 1], scale=cols["g1"][:, c:c + 1])
                        elif kind == "lin1":
                            ins = nc.scalar.activation(opT[:, j, 0:width], bank[4 + j][:, 0:width], ACT.Relu)
                        else:
                            ins = nc.scalar.activation(opT[:, j, 0:width], bank[4 + j][:, 0:width], ACT.Copy)
                        ins.then_inc(s_turned, 1)
                    if kind in FIRST_MID:
                        f = FIRST_MID.index(kind)
                        func, b = (ACT.Identity, "L1b") if kind == "mlp" else (ACT.Gelu, "L2b1")
                        for j in range(2):
                            act.wait_ge(s_m1, i * 2 + (NB * f + j + 1))
                            for c in range(KC):
                                ins = nc.scalar.activation(mid1[:, j, c * P:(c + 1) * P], bank[6 + j][:, c * P:(c + 1) * P], func,
                                                           bias=cols[b][:, c:c + 1])
                            ins.then_inc(s_m1o, 1)
                    if kind == "mlp":
                        for j in range(2):
                            act.wait_ge(s_m2, i * 2 + (j + 1))
                            for c in range(KC):
                                ins = nc.scalar.activation(mid2[:, j, c * P:(c + 1) * P], bank[2 + j][:, c * P:(c + 1) * P], ACT.Relu,
                                                           bias=cols["L1b1"][:, c:c + 1])
                            ins.then_inc(s_m2o, 1)

            norm(dis, 0)
            edge_pass(0)
            dense(0)
            edge_pass(1)
            dense(1)
            root(root_v[:, 0:NB], root_r[:, 0:NB])
            norm(diw, 1)
            edge_pass(2)
            dense(2)
            norm(None, 2)
            edge_pass(3)
            dense(3)
            root(root_v[:, 0:NB], root_r[:, 0:NB])
            dense(4)
            edge_pass(4)
            dense(5)
            edge_pass(5)

        @block.tensor
        def _(pe):
            pe.wait_ge(s_iota, 1)
            pe.wait_ge(s_pads, 1)
            pe.wait_ge(s_viol, 1)
            nc.tensor.matmul(bank[3][:, 0:1], ones[:], cnt[:, 0:1], start=True, stop=True).then_inc(s_violsum, 1)
            pe.wait_ge(s_flag, 1)
            mixed = pe.value_load(unsorted[0:1, 0:1], min_val=0, max_val=1)
            with pe.If(mixed < 1):
                pe.wait_ge(s_rows, 1)
                for n, t in enumerate((begun, step_f)):
                    for c in range(2):
                        ins = nc.tensor.matmul(bank[4 + 2 * n + c][:, 0:HW], ones[0:1, :], t[0:1, c * HW:c * HW + HW],
                                               start=True, stop=True)
                ins.then_inc(s_rowsout, 1)

            def degrees_open(b):
                nc.tensor.matmul(b[:, 0:NB], zero[:], zero[:, 0:NB], start=True, stop=False, skip_group_check=True)

            def degrees_add(b, ohl, ohh):
                for u in range(GROUP):
                    ins = nc.tensor.matmul(b[:, 0:NB], ohl[:, u * P:(u + 1) * P], ohh[:, u * NB:(u + 1) * NB],
                                           start=False, stop=False, skip_group_check=True)
                return ins

            def degrees_close(b):
                return nc.tensor.matmul(b[:, 0:NB], zero[:], zero[:, 0:NB], start=False, stop=True, skip_group_check=True)

            def bucket_sums(o):
                pe.wait_ge(s_cnt[o], 1)
                nc.tensor.matmul(bank[2][:, 0:NB], tri[:], cnt, start=True, stop=True)
                nc.tensor.matmul(bank[2][:, NB:2 * NB], ones[:], cnt, start=True, stop=True).then_inc(s_off[o], 1)

            degrees_open(bank[0])
            with pe.Fori(0, STEPS) as i:
                for h in range(2):
                    pe.wait_ge(s_oh[0], i * 2 + (h + 1))
                    degrees_add(bank[0], oh_low[h], oh_high[h]).then_inc(s_ohused[0], 1)
            degrees_close(bank[0]).then_inc(s_deg[0], 1)
            bucket_sums(1)
            with pe.If(mixed > 0):
                bucket_sums(0)
            with pe.Else():
                pe.wait_ge(s_lows, 1)
                for f, t in enumerate((run_f[0], run_f[1], run_i[2])):
                    for j in range(TW):
                        g = f * TW + j
                        ins = nc.tensor.transpose(bank[TURN[g // 4]][:, (g % 4) * P:(g % 4 + 1) * P],
                                                  t[:, j * P:(j + 1) * P], ident[:])
                ins.then_inc(s_runT, 1)

            def edge_pass(m):
                o, weighted, attrs = PASSES[m]

                def iteration(i, extra):
                    for k in range(RING):
                        if extra and m == 1 and k == HALF:
                            pe.wait_ge(s_oh[1], i + 1)
                            degrees_add(bank[7], oh1_low, oh1_high).then_inc(s_ohused[1], 1)
                        pe.wait_ge(s_onehot, i * RING + (T * m + k + 1))
                        if attrs:
                            pe.wait_ge(s_relu, i * RING + (k + 1))
                        else:
                            pe.wait_ge(s_gath[k], i * 16 + 16 * (ITER * m + 1))
                        pe.wait_ge(s_added, i * RING + (T * m + k + 1))
                        nc.tensor.matmul(bank[k % BANKS][:, 0:D], onehot[:, k, :], gbuf[:, k, :],
                                         start=True, stop=True).then_inc(s_tile, 1)

                lo = EXTRA.get(m, 0) if m == 1 else 0
                if lo:
                    degrees_open(bank[7])
                    with pe.Fori(0, lo) as i:
                        iteration(i, True)
                    degrees_close(bank[7]).then_inc(s_deg[1], 1)
                with pe.Fori(lo, ITER) as i:
                    iteration(i, False)

            def dense(q):
                kind = DENSE[q]
                if kind == "last":
                    return
                n = NB * q
                two = kind in ("gcn0", "gcn1")
                wa, wb, wc = {"gcn0": ("L0a", "L0r", None), "gcn1": ("L0b", "L0r", None), "mlp": ("L1b", "L1", "L1a"),
                              "gine": ("L2b", "L2a", None), "lin1": ("L3a", None, None), "lin2": ("L3b", None, None)}[kind]

                def middle(to, w, of):
                    for m_ in range(KC):
                        for k in range(KC):
                            ins = nc.tensor.matmul(to[:, m_ * P:(m_ + 1) * P], W[w][:, k, m_ * P:(m_ + 1) * P],
                                                   of[:, k * P:(k + 1) * P], start=(k == 0), stop=(k == KC - 1))
                    return ins

                with pe.Fori(0, BI) as i:
                    for j in range(2):
                        pe.wait_ge(s_op, i * 2 + (n + j + 1 + 2))
                        parts = [opa, opb] if two else [opa]
                        for s, t in enumerate(parts):
                            for c in range(KC):
                                at = (s * KC + c) * P
                                ins = nc.tensor.transpose(bank[4 + j][:, at:at + P], t[:, j, c * P:(c + 1) * P], ident[:])
                        ins.then_inc(s_turn, 1)
                    src = opT
                    if kind in FIRST_MID:
                        f = FIRST_MID.index(kind)
                        for j in range(2):
                            pe.wait_ge(s_turned, i * 2 + (n + j + 1))
                            middle(bank[6 + j], wb, opT[:, j, :]).then_inc(s_m1, 1)
                        src = mid1
                    if kind == "mlp":
                        for j in range(2):
                            pe.wait_ge(s_m1o, i * 2 + (j + 1))
                            middle(bank[2 + j], wc, mid1[:, j, :]).then_inc(s_m2, 1)
                        src = mid2
                    for j in range(2):
                        if kind == "mlp":
                            pe.wait_ge(s_m2o, i * 2 + (j + 1))
                        elif kind in FIRST_MID:
                            pe.wait_ge(s_m1o, i * 2 + (NB * f + j + 1))
                        else:
                            pe.wait_ge(s_turned, i * 2 + (n + j + 1))
                        ws = [wa, wb] if two else [wa]
                        for s, w in enumerate(ws):
                            for k in range(KC):
                                at = (s * KC + k) * P
                                ins = nc.tensor.matmul(bank[j][:, 0:D], src[:, j, at:at + P], W[w][:, k, :],
                                                       start=(s == 0 and k == 0), stop=(s == len(ws) - 1 and k == KC - 1))
                        ins.then_inc(s_pf, 1)

            pe.wait_ge(s_params, 16 * PARAMS)
            edge_pass(0)
            dense(0)
            edge_pass(1)
            dense(1)
            edge_pass(2)
            pe.wait_ge(s_late, 16 * 7)
            dense(2)
            edge_pass(3)
            dense(3)
            dense(4)
            edge_pass(4)
            dense(5)
            edge_pass(5)

        @block.vector
        def _(dve):
            link = Chain(dve, s_chain)
            V = nc.vector
            roots = [0]

            V.memset(zero[:], 0.0)
            for t in (src_i, dst_i, dst_next, dst1_i):
                V.memset(t[96:P, :], PAD_NODE)
            V.memset(pads[0], 0)
            V.memset(pads[1], -P * NB)
            V.memset(pads[2], 0.0)
            V.memset(weight1[96:P, :], 0.0)
            V.memset(weight[96:P, :], 0.0).then_inc(s_pads, 1)
            r3 = rec[:].rearrange("p (t f) -> p t f", f=FIELDS)
            link(V.memset(rec[:], 0.0))
            V.memset(r3[:, :, 1:2], -1.0).then_inc(s_unfilled, 1)
            V.memset(ones[:], 1.0).then_inc(s_ohused[0], 2)
            V.memset(tmpa[:], 0.0).then_inc(s_added, BANKS)
            V.memset(tmpb[:], 0.0).then_inc(s_row, 2)
            V.memset(mean[:], 0.0).then_inc(s_op, 2)
            V.memset(rstd[:], 0.0).then_inc(s_done, 2)
            V.memset(stats[:], 0.0).then_inc(s_ohused[1], 1)
            dve.wait_ge(s_iota, 1)
            dve.wait_ge(s_edges, 16 * 12)

            link(V.tensor_tensor(place, dst_i, dst_next, ALU.is_gt))
            V.tensor_reduce(cnt[:, 0:1], place, AX_X, ALU.add).then_inc(s_viol, 1)
            link(V.tensor_scalar(edge_no, edge_no, E - 1, None, ALU.min))
            dve.wait_ge(s_violsum, 1)
            V.tensor_scalar(unsorted[:], bank[3][:, 0:1], 1.0, None, ALU.min).then_inc(s_flag, 1)
            dve.wait_ge(s_flag, 1)
            mixed = dve.value_load(unsorted[0:1, 0:1], min_val=0, max_val=1)

            sl = Chain(dve, s_schain)
            with dve.If(mixed < 1):
                dve.wait_ge(s_ends, 64)
                row, begun_, step_, hit_ = place_i[0:1, :], begun[0:1, :], step_f[0:1, :], hit[0:1, :]
                sl(V.tensor_scalar(edge_ends, edge_ends, 7, None, ALU.logical_shift_right))
                sl(V.tensor_copy(begun_, edge_ends[:, 0:COLS]))
                sl(V.tensor_tensor(step_, edge_ends[:, COLS:], begun_, ALU.subtract))
                sl(V.tensor_scalar(step_, step_, 1.0, None, ALU.add))
                sl(V.tensor_tensor_scan(hit_, step_, step_, 0.0, ALU.add, ALU.max))
                sl(V.tensor_tensor(hit_, hit_, step_, ALU.subtract))
                sl(V.tensor_tensor(step_, begun_, hit_, ALU.subtract))
                sl(V.tensor_copy(place[0:1, :], step_))
                sl(V.tensor_copy(begun_, hit_))
                V.tensor_tensor(step_[:, 1:COLS], place[0:1, 1:COLS], place[0:1, 0:COLS - 1], ALU.subtract).then_inc(s_rows, 1)
                dve.wait_ge(s_rowsout, 1)
                for n, t in enumerate((begun, step_f)):
                    for c in range(2):
                        w = min(HW, COLS - c * HW)
                        ins = V.tensor_copy(t[:, c * HW:c * HW + w], bank[4 + 2 * n + c][:, 0:w])
                sl(ins)
                for j in range(TW):
                    sl(V.tensor_scalar(hit, begun, tile_no[:, j:j + 1], None, ALU.is_le, ALU.add, accum_out=t_chunk[:, j:j + 1]))
                    sl(V.tensor_tensor(hit, hit, step_f, ALU.mult))
                    sl(V.tensor_reduce(t_block[:, j:j + 1], hit, AX_X, ALU.add))
                sl(V.tensor_tensor(t_block, t_block, tile_no, ALU.add))
                sl(V.tensor_scalar(t_block, t_block, NB - 1.0, None, ALU.min))
                sl(V.tensor_scalar(t_base, t_block, float(P), None, ALU.mult))
                V.tensor_scalar(blk_i[0], t_block, float(D), None, ALU.mult)
                V.tensor_scalar(chunk_i, t_chunk, -1.0, None, ALU.add)
                sl(V.tensor_scalar(t_chunk, t_chunk, -1.0, float(P), ALU.add, ALU.mult))
                V.tensor_scalar(first_i, t_chunk, float(E - P), None, ALU.min).then_inc(s_tiles, 1)

            link(V.tensor_scalar(work_i, dst_i, P - 1, None, ALU.bitwise_and))
            link(V.tensor_copy(low_f, work_i))
            link(V.tensor_scalar(work_i, dst_i, 7, None, ALU.logical_shift_right))
            V.tensor_copy(high_b, work_i)
            link(V.tensor_copy(high_f, work_i))

            def degree_onehots(ohl, ohh, c, lows, highs, w, chain):
                V.tensor_tensor(ohl.rearrange("p (c n) -> p c n", n=P), iota_f[:].unsqueeze(1).to_broadcast([P, GROUP, P]),
                                lows[:, c].unsqueeze(2).to_broadcast([P, GROUP, P]), ALU.is_equal)
                high = ohh.rearrange("p (c n) -> p c n", n=NB)
                ins = V.tensor_tensor(high, iota_f[:, 0:NB].unsqueeze(1).to_broadcast([P, GROUP, NB]),
                                      highs[:, c].unsqueeze(2).to_broadcast([P, GROUP, NB]), ALU.is_equal)
                if w is not None:
                    chain(ins)
                    ins = V.tensor_tensor(high, high, w[:, c].unsqueeze(2).to_broadcast([P, GROUP, NB]), ALU.mult)
                return ins

            with dve.Fori(0, STEPS) as i:
                for h in range(2):
                    dve.wait_ge(s_ohused[0], i * 2 + (h + 1))
                    degree_onehots(oh_low[h], oh_high[h], bass.ds(i * (2 * GROUP) + h * GROUP, GROUP),
                                   low_f, high_f, None, None).then_inc(s_oh[0], 1)

            def bucket_counts(o, highs, junk, chain):
                with dve.Fori(0, BI) as i:
                    chain.enter(i, 2)
                    for j in range(2):
                        b = bass.ds(i * 2 + j, 1)
                        chain(V.tensor_scalar(junk, highs, iota_f[:, b], None, ALU.is_equal, ALU.add, accum_out=cnt[:, b]))
                    chain.leave(BI)
                V.memset(tmpa[:], 0.0).then_inc(s_cnt[o], 1)

            def bucket_places(o, chain):
                dve.wait_ge(s_off[o], 1)
                whole_i = whole.bitcast(I32)
                chain(V.tensor_scalar(whole_i, bank[2][:, NB:2 * NB], P - 1.0, None, ALU.add))
                chain(V.tensor_scalar(whole_i, whole_i, 7, None, ALU.logical_shift_right))
                chain(V.tensor_copy(tiles, whole_i))
                chain(V.tensor_tensor_scan(ends, tiles, zero[:, 0:NB], 0.0, ALU.add, ALU.add))
                chain(V.tensor_tensor(first, ends, tiles, ALU.subtract))
                chain(V.scalar_tensor_tensor(start[o], first, float(P), bank[2][:, 0:NB], ALU.mult, ALU.add))
                cmp = blk_cmp.rearrange("p (t b) -> p t b", b=NB)[:, :, 0:NB - 1]
                chain(V.tensor_tensor(cmp, tile_no.unsqueeze(2).to_broadcast([P, TW, NB - 1]),
                                      ends[:, 0:NB - 1].unsqueeze(1).to_broadcast([P, TW, NB - 1]), ALU.is_ge))
                chain(V.tensor_reduce(blk_f, cmp, AX_X, ALU.add))
                V.tensor_scalar(blk_i[o], blk_f, float(D), None, ALU.mult).then_inc(s_blk[o], 1)

            def bucket_scan(b, highs, msk, scn, plc, first_place, chain):
                chain(V.tensor_scalar(msk, highs, iota_f[:, bass.ds(b, 1)], None, ALU.is_equal))
                chain(V.tensor_tensor_scan(scn, msk, msk, first_place[:, bass.ds(b, 1)], ALU.add, ALU.max))
                chain(V.copy_predicated(plc, msk.bitcast(U16), scn))

            def to_rows(o, plc, wrk, rows_, chain):
                chain(V.tensor_scalar(wrk, plc, -1.0, None, ALU.add))
                chain(V.tensor_scalar(rows_, wrk, P - 1, None, ALU.bitwise_and))
                chain(V.tensor_scalar(wrk, wrk, 7, None, ALU.logical_shift_right))
                V.scalar_tensor_tensor(rows_, rows_, float(T), wrk, ALU.mult, ALU.add).then_inc(s_place[o], 1)

            spare_i = spare.bitcast(I32)
            link(V.tensor_scalar(spare_i, src_i, P - 1, None, ALU.bitwise_and))
            link(V.tensor_copy(low1, spare_i))
            link(V.tensor_scalar(spare_i, src_i, 7, None, ALU.logical_shift_right))
            link(V.tensor_copy(high1_b, spare_i))
            bucket_counts(1, high1_b, mask1, link)
            bucket_places(1, link)
            link(V.memset(place1, 0.0))

            with dve.If(mixed > 0):
                gl = Chain(dve, s_gchain)
                bucket_counts(0, high_b, mask, gl)
                bucket_places(0, gl)
                gl(V.memset(place, 0.0))
                with dve.Fori(0, NB) as i:
                    gl.enter(i, 3)
                    bucket_scan(i, high_b, mask, scan, place, start[0], gl)
                    gl.leave(NB)
                to_rows(0, place, work_i, place_i, gl)
                dve.wait_ge(s_place[0], 1)
                dve.wait_ge(s_blkst[0], 16)
                for h in range(2):
                    dve.wait_ge(s_scat[0][h], 16 * GROUP * STEPS)
                gl(V.memset(tmpb[:], 0.0))
            with dve.Else():
                dve.wait_ge(s_runs, 16 * 3 * TW)
                V.tensor_copy(run_f[0], run_i[0])
                for j in range(TW):
                    at = slice(j * P, (j + 1) * P)
                    ins = V.tensor_scalar(run_f[1][:, at], run_i[1][:, at], t_base[:, j:j + 1], None, ALU.subtract)
                ins.then_inc(s_lows, 1)
                dve.wait_ge(s_runT, 1)
                dve.wait_ge(s_prefill, 32)
                for f in range(3):
                    for j in range(TW):
                        g, n = f * TW + j, min(P, T - j * P)
                        ins = V.tensor_copy(r3[:, j * P:j * P + n, f], bank[TURN[g // 4]][:, (g % 4) * P:(g % 4) * P + n])
                ins.then_inc(s_built, 1)
                dve.wait_ge(s_built, 1)
                dve.wait_ge(s_blkst[0], 32)
                sl(V.memset(tmpb[:], 0.0))

            dve.wait_ge(s_deg[0], 1)
            dve.wait_ge(s_blkst[1], 16)
            link(V.tensor_scalar(dis[:], bank[0][:, 0:NB], 1.0, None, ALU.add))
            V.memset(onehot[:], 0.0).then_inc(s_tile, RING)
            link(V.memset(x_all[:, (N // P) * D:], 0.0))
            V.memset(fin[:], 0.0).then_inc(s_xfree, 1)

            roots = [0]

            def inverse_root(asked, w, to):
                roots[0] += 1
                asked.then_inc(s_root_in, 1)
                dve.wait_ge(s_root_out, roots[0])
                v, r, t = root_v[:, 0:w], root_r[:, 0:w], root_t[:, 0:w]
                link(V.reciprocal(r, r))
                link(V.tensor_tensor(t, v, r, ALU.mult))
                link(V.tensor_tensor(t, t, r, ALU.mult))
                link(V.tensor_scalar(t, t, -0.5, 1.5, ALU.mult, ALU.add))
                link(V.tensor_tensor(to, r, t, ALU.mult))

            dve.wait_ge(s_params, 16 * PARAMS)
            inverse_root(V.tensor_copy(root_v[:, 0:NB], dis[:]), NB, dis[:])
            link(V.tensor_tensor(sq[:], root_v[:, 0:NB], dis[:], ALU.mult))
            inverse_root(V.tensor_scalar(root_v[:, 0:KC], cols["var1"][:], EPS, None, ALU.add), KC, cols["var1"][:])
            link(V.tensor_tensor(cols["g1"][:], cols["g1"][:], cols["var1"][:], ALU.mult))
            link(V.tensor_tensor(cols["mu1"][:], cols["mu1"][:], cols["g1"][:], ALU.mult))
            link(V.tensor_tensor(cols["be1"][:], cols["be1"][:], cols["mu1"][:], ALU.subtract))
            inverse_root(V.tensor_scalar(root_v, rows["var2"][:], EPS, None, ALU.add), D, rows["var2"][:])
            link(V.tensor_tensor(rows["g2"][:], rows["g2"][:], rows["var2"][:], ALU.mult))
            link(V.tensor_tensor(rows["L2b2"][:], rows["L2b2"][:], rows["mu2"][:], ALU.subtract))
            link(V.tensor_tensor(rows["L2b2"][:], rows["L2b2"][:], rows["g2"][:], ALU.mult))
            link(V.tensor_tensor(rows["be2"][:], rows["be2"][:], rows["L2b2"][:], ALU.add))
            link(V.tensor_tensor(rows["L0a"][:], rows["L0a"][:], rows["L0r"][:], ALU.add))
            link(V.tensor_tensor(rows["L0b"][:], rows["L0b"][:], rows["L0r"][:], ALU.add))
            dve.wait_ge(s_nodes, 32 if N % P else 16)

            def weighted_factors():
                dve.wait_ge(s_deg[1], 1)
                link(V.tensor_scalar(diw[:], bank[7][:, 0:NB], 1.0, None, ALU.add))
                link(V.tensor_scalar(tmpa[:], diw[:], 0.0, None, ALU.is_gt))
                inverse_root(V.tensor_scalar(root_v[:, 0:NB], diw[:], 1e-30, None, ALU.max), NB, diw[:])
                link(V.tensor_tensor(diw[:], diw[:], tmpa[:], ALU.mult))

            def statistics():
                with dve.Fori(0, BI) as i:
                    for j in range(2):
                        b = i * 2 + j
                        V.bn_stats(stats[:, bass.ds(b * 6, 6)], blk(x_all, b))
                st = stats[:].rearrange("p (b s) -> p b s", s=6)
                link(V.memset(tmpb[:], 0.0))
                link(V.tensor_tensor(tmpa[:], st[:, :, 1], st[:, :, 4], ALU.add))
                link(V.tensor_scalar(mean[:], tmpa[:], 0.5, None, ALU.mult))
                link(V.tensor_tensor(tmpa[:], st[:, :, 1], st[:, :, 4], ALU.subtract))
                link(V.scalar_tensor_tensor(tmpa[:], tmpa[:], 0.25, tmpa[:], ALU.mult, ALU.mult))
                link(V.tensor_tensor(tmpb[:], st[:, :, 2], st[:, :, 5], ALU.add))
                link(V.scalar_tensor_tensor(tmpa[:], tmpb[:], 1.0 / D, tmpa[:], ALU.mult, ALU.add))
                inverse_root(V.tensor_scalar(root_v[:, 0:NB], tmpa[:], EPS, None, ALU.add), NB, rstd[:])

            def norm(made):
                statistics()
                with dve.Fori(0, BI) as i:
                    for j in range(2):
                        b = i * 2 + j
                        dve.wait_ge(s_row, i * 2 + (NB * made + j + 1))
                        V.tensor_scalar(opa[:, j, :], blk(x_all, b), mean[:, bass.ds(b, 1)], rstd[:, bass.ds(b, 1)],
                                        ALU.subtract, ALU.mult).then_inc(s_z, 1)

            def edge_pass(m):
                o, weighted, attrs = PASSES[m]
                dve.wait_ge(s_recld, 32 * [1, 1, 2, 3, 3, 3][m])
                dve.wait_ge(s_tabst, 16 * (m + 1))

                def onehots(i, h):
                    dve.wait_ge(s_staged, i * 2 + (2 * ITER * m + h + 1))
                    lows = low[:, h, :].rearrange("p (t f) -> p t f", f=2)
                    if not weighted:
                        V.tensor_tensor(onehot[:, h * HALF:(h + 1) * HALF, :], iota_f[:].unsqueeze(1).to_broadcast([P, HALF, P]),
                                        lows[:, :, 0:1].to_broadcast([P, HALF, P]), ALU.is_equal).then_inc(s_onehot, HALF)
                        return
                    for u in range(HALF):
                        V.tensor_scalar(onehot[:, h * HALF + u, :], iota_f[:], lows[:, u, 0:1], lows[:, u, 1:2],
                                        ALU.is_equal, ALU.mult).then_inc(s_onehot, 1)

                def message(i, k):
                    dve.wait_ge(s_gath[k], i * 16 + 16 * (ITER * m + 1))
                    dve.wait_ge(s_egath[k], i * 16 + 16)
                    V.tensor_tensor(gbuf[:, k, :], gbuf[:, k, :], ebuf[:, k, :], ALU.add).then_inc(s_msg, 1)

                columns = [None] * LOADS

                def add(i, k):
                    if k % LOADS == 0:
                        columns[:] = load_row(row0, i * RING + k, mybir.EngineType.DVE, (NB - 1) * D)
                    to = acc[:, bass.ds(columns[k % LOADS], D)]
                    dve.wait_ge(s_tile, i * RING + (T * m + k + 1 + RING))
                    dve.wait_ge(s_added, i * RING + (T * m + k + BANKS))
                    V.tensor_tensor(to, to, bank[k % BANKS][:, 0:D], ALU.add).then_inc(s_added, 1)

                lag = LAG if attrs else 0

                def iteration(i, extra=False, begins=False, ends=False):
                    for k in range(RING):
                        if k == 0:
                            onehots(i, 1)
                            if extra and m == 0:
                                bucket_scan(i, high1_b, mask1, scan1, place1, start[1], link)
                            if extra and m == 1:
                                dve.wait_ge(s_ohused[1], i + 1)
                                degree_onehots(oh1_low, oh1_high, bass.ds(i * GROUP, GROUP), low1, high1_b, weight,
                                               link).then_inc(s_oh[1], 1)
                        if k == HALF and not ends:
                            onehots(i + 1, 0)
                        if attrs:
                            message(i, k)
                        if not (begins and k < lag):
                            add(i, k - lag)
                    if ends:
                        for k in range(RING - lag, RING):
                            add(i, k)

                lo = EXTRA.get(m, 0)
                onehots(0, 0)
                if lo:
                    with dve.Fori(0, lo) as i:
                        link.enter(i, (3, 1)[m])
                        iteration(i, extra=True)
                        link.leave(lo)
                elif lag:
                    iteration(0, begins=True)
                    lo = 1
                if lo < ITER - 1:
                    with dve.Fori(lo, ITER - 1) as i:
                        iteration(i)
                iteration(ITER - 1, ends=True)
                if m == 0:
                    to_rows(1, place1, spare_i, place1_i, link)
                    dve.wait_ge(s_place[1], 1)

            def dense(q):
                kind = DENSE[q]
                n = NB * q
                dve.wait_ge(s_added, T * {"gcn0": 1, "gcn1": 2, "mlp": 3, "gine": 4, "lin1": 4, "lin2": 5, "last": 6}[kind] + BANKS)
                dve.wait_ge(s_done, n + 2)
                row = {"gcn0": "L0a", "gcn1": "L0b", "mlp": "L1b2", "lin1": "L3b1", "lin2": "L3b2"}.get(kind)
                with dve.Fori(0, BI) as i:
                    steps = {"gcn0": 1, "gcn1": 1, "mlp": 1, "gine": 3, "lin1": 1, "lin2": 1, "last": 1}[kind]
                    link.enter(i, steps)
                    bs = [i * 2, i * 2 + 1]
                    col = [bass.ds(b, 1) for b in bs]
                    if kind != "last":
                        for j in range(2):
                            a = blk(acc, bs[j])
                            dve.wait_ge(s_done, i * 2 + (n + j + 1))
                            if kind in READS_TABLE:
                                dve.wait_ge(s_tin[j], i * 16 + 16 * (BI * READS_TABLE.index(kind) + 1))
                            if kind in ("gcn0", "gcn1"):
                                V.tensor_scalar(opa[:, j, :], a, dis[:, col[j]], None, ALU.mult)
                                ins = V.tensor_scalar(opb[:, j, :], tin[:, j, :], sq[:, col[j]], None, ALU.mult)
                            elif kind == "mlp":
                                ins = V.tensor_scalar(opa[:, j, :], a, diw[:, col[j]], None, ALU.mult)
                            elif kind == "gine":
                                ins = V.tensor_tensor(opa[:, j, :], a, tin[:, j, :], ALU.add)
                            elif kind == "lin1":
                                ins = V.tensor_scalar(opa[:, j, :], blk(x_all, bs[j]), mean[:, col[j]], rstd[:, col[j]],
                                                      ALU.subtract, ALU.mult)
                            else:
                                ins = V.tensor_scalar(opa[:, j, :], a, dis[:, col[j]], 0.0, ALU.mult, ALU.max)
                            ins.then_inc(s_op, 1)

                    def first(j):
                        if kind == "last":
                            dve.wait_ge(s_done, i * 2 + (n + j + 1))
                            return V.tensor_scalar(fin[:, j, :], blk(acc, bs[j]), dis[:, col[j]], 0.0, ALU.mult, ALU.max)
                        dve.wait_ge(s_pf, i * 2 + (n + j + 1))
                        return V.tensor_tensor(fin[:, j, :], bank[j][:, 0:D], opa[:, j, :] if kind == "gine" else rows[row][:], ALU.add)

                    first(0)
                    link(first(1))
                    if kind == "gine":
                        for op, r in ((ALU.mult, "g2"), (ALU.add, "be2")):
                            V.tensor_tensor(fin[:, 0, :], fin[:, 0, :], rows[r][:], op)
                            link(V.tensor_tensor(fin[:, 1, :], fin[:, 1, :], rows[r][:], op))
                    for j in range(2):
                        xb, ab = blk(x_all, bs[j]), blk(acc, bs[j])
                        if kind == "gcn0":
                            ins = V.tensor_scalar(ab, fin[:, j, :], dis[:, col[j]], 0.0, ALU.mult, ALU.max)
                        elif kind in ("lin1", "lin2"):
                            ins = V.tensor_scalar(ab, fin[:, j, :], dis[:, col[j]], None, ALU.mult)
                        elif kind == "gcn1":
                            ins = V.scalar_tensor_tensor(xb, fin[:, j, :], 0.0, xb, ALU.max, ALU.add)
                        else:
                            ins = V.tensor_tensor(xb, xb, fin[:, j, :], ALU.add)
                        ins.then_inc(s_done, 1)
                    link.leave(BI)
                dve.wait_ge(s_done, n + NB + 2)

            norm(0)
            edge_pass(0)
            dense(0)
            edge_pass(1)
            dense(1)
            weighted_factors()
            norm(1)
            edge_pass(2)
            dense(2)
            norm(2)
            edge_pass(3)
            dense(3)
            statistics()
            dense(4)
            edge_pass(4)
            dense(5)
            edge_pass(5)
            dense(6)


_INS = ["x", "src", "dst", "edge_attr_256", "edge_weight", "edge_weight1",
        "L0_gnn_W", "L0_gnn_b", "L0_gnn_resW", "L0_gnn_resb",
        "L1_gnn_W", "L1_gnn_b", "L1_gnn_W1", "L1_gnn_b1", "L1_gnn_W2", "L1_gnn_b2",
        "L2_gnn_W1", "L2_gnn_b1", "L2_gnn_W2", "L2_gnn_b2",
        "L2_gnn_bn1_gamma", "L2_gnn_bn1_beta", "L2_gnn_bn1_mean", "L2_gnn_bn1_var",
        "L2_gnn_bn2_gamma", "L2_gnn_bn2_beta", "L2_gnn_bn2_mean", "L2_gnn_bn2_var",
        "L3_gnn_W1", "L3_gnn_b1", "L3_gnn_W2", "L3_gnn_b2"]
_TURNED = ("L2_gnn_W1", "L2_gnn_W2", "L3_gnn_W1", "L3_gnn_W2")


def kernel(**inputs):
    import numpy as np
    import concourse.bacc as bacc
    from concourse.bass_utils import run_bass_kernel_spmd

    nc = bacc.Bacc("TRN2", target_bir_lowering=False, num_devices=1)
    arrays, io = {}, {}
    for name in _INS:
        a = np.asarray(inputs[name])
        a = np.ascontiguousarray(a.T if name in _TURNED else a)
        arrays[f"in_{name}"] = a
        io[name] = nc.dram_tensor(f"in_{name}", a.shape, mybir.dt.from_np(a.dtype), kind="ExternalInput").ap()
    out = nc.dram_tensor("out_0", io["x"].shape, F32, kind="ExternalOutput").ap()
    build(nc, io, out)
    r = run_bass_kernel_spmd(nc, [arrays], core_ids=[0])
    return r.results[0]["out_0"]
```

```python
from contextlib import ExitStack

import concourse.bass as bass
from concourse import mybir

P = 128
F32 = mybir.dt.float32
BF16 = mybir.dt.bfloat16
I32 = mybir.dt.int32
U16 = mybir.dt.uint16
ALU = mybir.AluOpType
ACT = mybir.ActivationFunctionType
AX_X = mybir.AxisListType.X
EPS = 1e-5

HALF = 8
RING = 2 * HALF
LAG = 4
BANKS = 4
LOADS = 4


class Chain:

    def __init__(self, eng, sem):
        self.eng, self.sem, self.n, self.i, self.per = eng, sem, 0, None, 0

    def __call__(self, ins):
        self.n += 1
        ins.then_inc(self.sem, 1)
        self.eng.wait_ge(self.sem, self.n if self.i is None else self.i * self.per + self.n)
        if self.i is not None:
            self.eng.nop(nofuse=True)

    def enter(self, i, per):
        self.i, self.per, self.start = i, per, self.n

    def leave(self, iterations):
        assert self.n - self.start == self.per
        self.n += self.per * (iterations - 1)
        self.i = None


def build(nc, io, out):
    N, D = io["x"].shape
    E = io["src"].shape[0]
    KC = D // P
    NB = -(-N // P)
    NB += NB % 2
    if NB * P == N:
        NB += 2
    COLS = -(-E // P)
    PAD_NODE = (NB - 1) * P
    T = (COLS * P + NB * (P - 1)) // P
    T = -(-T // RING) * RING
    GROUP = next(g for g in range(20, 0, -1) if COLS % (2 * g) == 0)
    STEPS = COLS // (2 * GROUP)
    TW = -(-T // P)
    FIELDS = 4
    LAST = E - (P - 1) * COLS
    assert (NB - 1) * P >= N and 0 < LAST <= COLS and D == KC * P

    with ExitStack() as ctx:
        def sb(name, shape, dt=F32):
            return ctx.enter_context(nc.sbuf_tensor(name, shape, dt))

        def sem(name):
            return ctx.enter_context(nc.semaphore(name))

        table = nc.dram_tensor("table", (NB * P, D), F32, kind="Internal").ap()
        records = [nc.dram_tensor(f"records{o}", (P * T, FIELDS), F32, kind="Internal").ap() for o in range(2)]
        blockrow = [nc.dram_tensor(f"blockrow{o}", (P * TW,), I32, kind="Internal").ap() for o in range(2)]
        startrow = nc.dram_tensor("startrow", (P * TW,), I32, kind="Internal").ap()
        chunks = [nc.dram_tensor(f"chunks{f}", (COLS, P), (I32, I32, F32)[f], kind="Internal").ap() for f in range(3)]

        x_all = sb("x_all", [P, NB * D])
        acc = sb("acc", [P, NB * D])
        rec = sb("rec", [P, T * FIELDS])
        row0 = sb("row0", [1, T], I32)
        first_edge = sb("first_edge", [1, T], I32)
        unsorted = sb("unsorted", [P, 1], I32)
        gbuf = sb("gbuf", [P, RING, D])
        ebuf = sb("ebuf", [P, RING, D])
        onehot = sb("onehot", [P, RING, P])
        idx = sb("idx", [P, 2, HALF], I32)
        eidx = sb("eidx", [P, 2, HALF], I32)
        low = sb("low", [P, 2, HALF * 2])

        iota_f = sb("iota_f", [P, P])
        iota_b = sb("iota_b", [P, P], BF16)
        ident = sb("ident", [P, P])
        tri = sb("tri", [P, P])
        ones = sb("ones", [P, P])
        zero = sb("zero", [P, P])
        w_late = sb("w_late", [P, 7, KC, D])
        W = {k: sb("w_" + k, [P, KC, D])[:] for k in ("L0a", "L0b", "L0r")}
        W.update({k: w_late[:, n] for n, k in enumerate(("L1", "L1a", "L1b", "L2a", "L2b", "L3a", "L3b"))})
        rows = {k: sb("row_" + k, [P, D]) for k in
                ("L0a", "L0b", "L1b2", "L3b1", "L3b2", "g2", "be2")}
        cols = {k: sb("col_" + k, [P, KC]) for k in ("L1b", "L1b1", "L2b1", "g1", "be1", "mu1", "var1")}
        stats = sb("stats", [P, NB * 6])
        mean, rstd = sb("mean", [P, NB]), sb("rstd", [P, NB])
        tmpa, tmpb = sb("tmpa", [P, NB]), sb("tmpb", [P, NB])
        dis, sq, diw = sb("dis", [P, NB]), sb("sq", [P, NB]), sb("diw", [P, NB])

        tin = sb("tin", [P, 2, D])
        opa, opb = sb("opa", [P, 2, D]), sb("opb", [P, 2, D])
        opT = sb("opT", [P, 2, 2 * D])
        root_v, root_r, root_t = opT[:, 0, 0:D], opT[:, 0, D:2 * D], opT[:, 1, 0:D]
        mid = opb
        fin = sb("fin", [P, 2, D])
        normed = [opa[:, 0, :], opa[:, 1, :], fin[:, 0, :], fin[:, 1, :]]
        rows.update({"L0r": opb[:, 0, :], "mu2": opb[:, 1, :], "var2": tin[:, 0, :], "L2b2": tin[:, 1, :]})

        class Lent:

            def __init__(self, t):
                self.t, self.at = t, 0

            def __call__(self, words, dt=F32):
                a = self.t[:, self.at:self.at + words]
                self.at += words
                assert self.at <= self.t.shape[1]
                return a if dt == F32 else a.bitcast(dt)

        HW = -(-COLS // 2)
        lend = Lent(acc[:])
        src_i, dst_i, dst_next = (lend(COLS, I32) for _ in range(3))
        weight1, edge_no = lend(COLS), lend(COLS, I32)
        low_f, high_f, high_b = lend(COLS), lend(COLS), lend(HW, BF16)[:, 0:COLS]
        work_i, place, place_i = lend(COLS, I32), lend(COLS), lend(COLS, I32)
        mask = lend(HW, BF16)[:, 0:COLS]
        begun, step_f, hit = lend(COLS), lend(COLS), lend(COLS)
        low_b = dst_next.bitcast(BF16)[:, 0:COLS]
        run_f = [lend(TW * P) for _ in range(2)]
        lend = Lent(onehot[:].rearrange("p r n -> p (r n)"))
        run_i = [lend(TW * P, I32), lend(TW * P, I32)]
        run_i.append(opT[:].rearrange("p j d -> p (j d)")[:, 0:TW * P])
        lend = Lent(gbuf[:].rearrange("p r d -> p (r d)"))
        oh_low = [lend(GROUP * P // 2, BF16) for _ in range(2)]
        oh_high = [lend(GROUP * NB // 2, BF16) for _ in range(2)]
        PADS = COLS * P - E
        lend = Lent(ebuf[:].rearrange("p r d -> p (r d)"))
        dst1_i, low1, weight, place1_i = lend(COLS, I32), lend(COLS), lend(COLS), lend(COLS, I32)
        high1_b = lend(HW, BF16)[:, 0:COLS]
        lend = Lent(w_late[:].rearrange("p a k d -> p (a k d)"))
        place1, scan1 = lend(COLS), lend(COLS)
        spare = lend(COLS)
        mask1 = lend(HW, BF16)[:, 0:COLS]
        blk_cmp, blk_f = lend(TW * NB), lend(TW)
        pads = [lend(PADS, (I32, I32, F32)[f])[0:1, :] for f in range(3)]
        flat = w_late[:].rearrange("p a k d -> p (a k d)")
        edge_ends = flat[0:1, 0:2 * COLS].bitcast(I32)
        lend = Lent(gbuf[:].rearrange("p r d -> p (r d)"))
        oh1_low = [flat[:, 0:GROUP * P], lend(GROUP * P)]
        oh1_high = [flat[:, 3 * COLS:3 * COLS + GROUP * NB], lend(GROUP * NB)]
        scan = onehot[:].rearrange("p r n -> p (r n)")[:, 0:COLS]
        small = sb("small", [P, 8 * NB])
        cnt, first, tiles, ends, whole = (small[:, k * NB:(k + 1) * NB] for k in range(5))
        cnts = [cnt, small[:, 7 * NB:8 * NB]]
        start = [small[:, (5 + o) * NB:(6 + o) * NB] for o in range(2)]
        tabs = sb("tabs", [P, 8 * TW])
        tile_no, t_chunk, t_block, t_base = (tabs[:, k * TW:(k + 1) * TW] for k in range(4))
        blk_i = [tabs[:, (4 + o) * TW:(5 + o) * TW].bitcast(I32) for o in range(2)]
        chunk_i, first_i = (tabs[:, k * TW:(k + 1) * TW].bitcast(I32) for k in (6, 7))
        stage_idx = sb("stage_idx", [P, 2, GROUP], I32)
        stage_rec = sb("stage_rec", [P, 2, GROUP * FIELDS])

        bank = [ctx.enter_context(nc.psum_tensor(f"bank{k}", [P, 512], F32)) for k in range(8)]

        TURN = (4, 5, 6, 7, 1, 3)

        s_achain = sem("scalar_chain")
        s_buckets = sem("buckets_of_sources")
        s_pads, s_iota, s_unfilled, s_xfree = (sem(k) for k in ("pads_written", "constants_ready", "unfilled_ready", "x_free"))
        s_edges, s_ends, s_chunks = sem("edges_loaded"), sem("run_ends_loaded"), sem("runs_laid_out")
        s_nodes, s_params, s_late = sem("nodes_loaded"), sem("params_loaded"), sem("late_weights_loaded")
        s_chain, s_pchain = sem("vector_chain"), sem("pool_chain")
        s_gchain, s_schain = sem("vector_chain_general"), sem("vector_chain_sorted")
        s_spchain = [sem(f"pool_staged_order{o}") for o in range(2)]
        s_root_in, s_root_out = sem("root_asked"), sem("root_taken")
        s_viol, s_violsum, s_flag = sem("inversions_ready"), sem("inversions_summed"), sem("unsorted_known")
        s_rows, s_rowsout = sem("run_tables_ready"), sem("run_tables_spread")
        s_tiles, s_runs, s_lows = sem("tile_tables_ready"), sem("runs_gathered"), sem("run_places_ready")
        s_runT, s_built, s_recst = sem("runs_turned"), sem("records_built"), sem("records_stored")
        s_oh, s_ohused = ([sem(f"degree_onehots_{k}{o}") for o in range(2)] for k in ("ready", "used"))
        s_deg = [sem(f"degrees_ready{o}") for o in range(2)]
        s_cnt0, s_off = sem("counts_ready0"), [sem(f"offsets_ready{o}") for o in range(2)]
        s_batchnorms, s_term = sem("batchnorms_ready"), sem("batchnorm_term_added")
        s_foldT, s_foldTo, s_foldP, s_mlp = (sem(k) for k in ("weights_turned", "turned_weights_copied", "weights_multiplied",
                                                              "mlp_weights_ready"))
        s_prefill, s_place = sem("records_prefilled"), [sem(f"places_ready{o}") for o in range(2)]
        s_blk, s_blkst = ([sem(f"blocks_{k}{o}") for o in range(2)] for k in ("ready", "stored"))
        s_scat = [[sem(f"scattered{o}{h}") for h in range(2)] for o in range(2)]
        s_recld = sem("records_loaded")
        s_staged = sem("indices_staged")
        s_gath = [sem(f"gathered{k}") for k in range(RING)]
        s_egath = [sem(f"edges_gathered{k}") for k in range(RING)]
        s_msg, s_relu = sem("messages_added"), sem("messages_ready")
        s_onehot, s_tile, s_added = sem("onehot_ready"), sem("tile_summed"), sem("tile_added")
        s_z, s_row = sem("normalized"), sem("table_rows_ready")
        s_tabst = sem("table_stored")
        s_tin = [sem(f"table_block{k}_loaded") for k in range(2)]
        s_op, s_turn, s_turned = sem("operands_ready"), sem("operands_turned"), sem("turned_copied")
        s_m, s_mo = sem("middle_product"), sem("middle_copied")
        s_pf, s_fin, s_done = sem("last_product"), sem("last_product_taken"), sem("block_done")
        s_res, s_folded = sem("residual_ready"), sem("batchnorm_folded")
        s_out = sem("output_stored")

        PASSES = [(0, False, False), (0, False, False), (1, True, False),
                  (0, False, True), (0, True, False), (0, True, False)]
        DENSE = ["gcn0", "gcn1", "mlp", "gine", "lin1", "lin2", "last"]
        READS_TABLE = ["gcn0", "gcn1", "gine"]
        MIDDLE = ["mlp", "gine"]
        ITER = T // RING
        BI = NB // 2
        PIECES = next(c for c in range(6, 0, -1) if NB % c == 0)
        PART = 14
        PARAMS = 3 + 11 + 7
        EXTRA = {0: NB}
        assert NB < ITER and 0 < PART < STEPS

        class At:

            def __init__(self, i, off, per=2):
                self.i, self.off, self.per, self.j = i, off, per, off % 2

            def __add__(self, c):
                return self.off + c if self.i is None else self.i * self.per + (self.off + c)

            def cols(self, t, width):
                at = self.off * width if self.i is None else self.i * (self.per * width) + self.off * width
                return t[:, bass.ds(at, width)]

        def pairs(eng, step):
            with eng.Fori(0, BI) as i:
                for j in range(2):
                    step(At(i, j))

        def fours(eng, step):
            for b in range(4):
                step(At(None, b))
            with eng.Fori(1, NB // 4) as i:
                for j in range(4):
                    step(At(i, j, 4))
            for b in range(NB - NB % 4, NB):
                step(At(None, b))

        def pipeline(eng, stages):
            deepest = max(lag for lag, _ in stages)
            head = 2 * -(-deepest // 2)

            def step(i, t):
                for lag, what in stages:
                    if what is not None and (i is not None or 0 <= t - lag < NB):
                        what(At(i, t - lag))

            for t in range(head):
                step(None, t)
            with eng.Fori(head // 2, BI) as i:
                for j in range(2):
                    step(i, j)
            for t in range(NB, NB + deepest):
                step(None, t)

        TURN_LAG, MID_LAG = 1, 2
        LAST_LAG = {"gcn0": 2, "gcn1": 2, "mlp": 3, "gine": 3, "lin1": 2, "lin2": 2}
        WITH_STATS = ["gcn1", "mlp", "gine"]

        def deepest(kind):
            return (LAST_LAG[kind] + (2 if kind in WITH_STATS else 1), None)

        def load_row(t, at, engine, most):
            return nc.values_load_multi_w_load_instructions(
                t[0:1, bass.ds(at, LOADS)], engines=(engine,), min_val=0, max_val=most,
                skip_runtime_bounds_check_because="VectorE has cut the values to their range")[1]

        block = ctx.enter_context(nc.Block())

        @block.sync
        def _(sp):
            sp.wait_ge(s_pads, 1)
            ew1 = io["edge_weight1"].rearrange("e a -> (e a)")
            for to, a, n in ((dst_i, io["dst"], E), (dst_next, io["dst"][1:E], E - 1), (src_i, io["src"], E), (weight1, ew1, E),
                             (weight, io["edge_weight"], E), (dst1_i, io["dst"], E)):
                sp.dma_start(to[0:P - 1, :], a[0:(P - 1) * COLS].rearrange("(p c) -> p c", c=COLS)).then_inc(s_edges, 16)
                left = n - (P - 1) * COLS
                sp.dma_start(to[P - 1:P, 0:left], a[(P - 1) * COLS:n].rearrange("(p c) -> p c", p=1)).then_inc(s_edges, 16)
            whole_runs = (COLS - 1) * P
            with nc.allow_non_contiguous_dma(reason="one element of each run of 128 edges"):
                for k, at in enumerate((0, P - 1)):
                    sp.dma_start(edge_ends[:, k * COLS:(k + 1) * COLS - 1],
                                 io["dst"][0:whole_runs].rearrange("(a c e) -> a c e", e=P, a=1)[:, :, at]).then_inc(s_ends, 16)
                for k, at in enumerate((whole_runs, E - 1)):
                    sp.dma_start(edge_ends[:, (k + 1) * COLS - 1:(k + 1) * COLS],
                                 io["dst"][at:at + 1].rearrange("(a c) -> a c", a=1)).then_inc(s_ends, 16)
            for f, a in enumerate((io["src"], io["dst"], ew1)):
                sp.dma_start(chunks[f][0:COLS - 1], a[0:whole_runs].rearrange("(c e) -> c e", e=P)).then_inc(s_chunks, 16)
                sp.dma_start(chunks[f][COLS - 1:COLS, 0:PADS], pads[f]).then_inc(s_chunks, 16)
                sp.dma_start(chunks[f][COLS - 1:COLS, PADS:P], a[whole_runs:E].rearrange("(c e) -> c e", c=1)).then_inc(s_chunks, 16)
            sp.wait_ge(s_unfilled, 1)
            for o in range(2):
                sp.dma_start(records[o].rearrange("(p t) f -> p (t f)", p=P), rec[:]).then_inc(s_prefill, 16)
            for k, a in (("L0a", io["L0_gnn_W"][0]), ("L0b", io["L0_gnn_W"][1]), ("L0r", io["L0_gnn_resW"])):
                sp.dma_start(W[k], a.rearrange("(k p) n -> p k n", p=P)).then_inc(s_params, 16)
            for k, a in (("L0a", io["L0_gnn_b"][0]), ("L0b", io["L0_gnn_b"][1]), ("L0r", io["L0_gnn_resb"]),
                         ("L1b2", io["L1_gnn_b2"]), ("L3b1", io["L3_gnn_b1"]), ("L3b2", io["L3_gnn_b2"]),
                         ("g2", io["L2_gnn_bn2_gamma"]), ("be2", io["L2_gnn_bn2_beta"]), ("mu2", io["L2_gnn_bn2_mean"]),
                         ("var2", io["L2_gnn_bn2_var"]), ("L2b2", io["L2_gnn_b2"])):
                sp.dma_start(rows[k][:], a.partition_broadcast(P)).then_inc(s_params, 16)
            with nc.allow_non_contiguous_dma(reason="seven vectors of 256, one element per partition"):
                for k, a in (("L1b", io["L1_gnn_b"]), ("L1b1", io["L1_gnn_b1"]), ("L2b1", io["L2_gnn_b1"]),
                             ("g1", io["L2_gnn_bn1_gamma"]), ("be1", io["L2_gnn_bn1_beta"]),
                             ("mu1", io["L2_gnn_bn1_mean"]), ("var1", io["L2_gnn_bn1_var"])):
                    sp.dma_start(cols[k][:], a.rearrange("(m p) -> p m", p=P)).then_inc(s_params, 16)

            sp.wait_ge(s_xfree, 1)
            full = N // P
            sp.dma_start(x_all[:, 0:full * D].rearrange("p (b d) -> p b d", d=D),
                         io["x"][0:full * P].rearrange("(b p) d -> p b d", p=P)).then_inc(s_nodes, 16)
            if N % P:
                sp.dma_start(x_all[0:N % P, full * D:(full + 1) * D], io["x"][full * P:N]).then_inc(s_nodes, 16)

            def by_tile(dram):
                return dram.rearrange("(j p) -> p j", p=P)

            def as_row(dram):
                return dram[0:T].rearrange("(a t) -> a t", a=1)

            with nc.allow_non_contiguous_dma(reason="seven words per partition, in tiles' order"):
                sp.wait_ge(s_blk[1], 1)
                sp.dma_start(by_tile(blockrow[1]), blk_i[1]).then_inc(s_blkst[1], 16)
                sp.wait_ge(s_flag, 1)
                mixed = sp.value_load(unsorted[0:1, 0:1], min_val=0, max_val=1)
                with sp.If(mixed > 0):
                    sp.wait_ge(s_ends, 64)
                    sp.wait_ge(s_chunks, 16 * 9)
                    sp.wait_ge(s_blk[0], 1)
                    sp.dma_start(by_tile(blockrow[0]), blk_i[0]).then_inc(s_blkst[0], 16)
                    sp.wait_ge(s_blkst[0], 16)
                    for h in range(2):
                        sp.wait_ge(s_scat[0][h], 16 * GROUP * STEPS)
                    sp.dma_start(rec[:], records[0].rearrange("(p t) f -> p (t f)", p=P)).then_inc(s_recld, 16)
                    sp.dma_start(row0[:], as_row(blockrow[0])).then_inc(s_recld, 16)
                with sp.Else():
                    sp.wait_ge(s_tiles, 1)
                    sp.dma_start(by_tile(blockrow[0]), blk_i[0]).then_inc(s_blkst[0], 16)
                    sp.dma_start(by_tile(startrow), first_i).then_inc(s_blkst[0], 16)
                    sp.wait_ge(s_blkst[0], 32)
                    sp.dma_start(first_edge[:], as_row(startrow)).then_inc(s_recld, 16)
                    sp.wait_ge(s_built, 1)
                    sp.dma_start(records[0].rearrange("(p t) f -> p (t f)", p=P), rec[:]).then_inc(s_recst, 16)
                    sp.dma_start(row0[:], as_row(blockrow[0])).then_inc(s_recld, 16)
                    sp.wait_ge(s_recst, 16)
            table_b = table.rearrange("(b p) d -> p b d", p=P)

            def load_records(o):
                sp.dma_start(rec[:], records[o].rearrange("(p t) f -> p (t f)", p=P)).then_inc(s_recld, 16)
                sp.dma_start(row0[:], as_row(blockrow[o])).then_inc(s_recld, 16)

            def store_table(made, before):
                n = NB // PIECES
                for c in range(PIECES):
                    sp.wait_ge(made, before + (c + 1) * n)
                    sp.dma_start(table_b[:, c * n:(c + 1) * n], acc[:, c * n * D:(c + 1) * n * D].rearrange("p (b d) -> p b d", d=D)
                                 ).then_inc(s_tabst, 16)

            def load_edges(m):
                with sp.Fori(0, ITER) as i:
                    for k in range(RING):
                        if k % LOADS == 0:
                            starts = load_row(first_edge, i * RING + k, mybir.EngineType.SP, E - P)
                        e = starts[k % LOADS]
                        sp.wait_ge(s_tile, i * RING + (T * m + k + 1))
                        sp.nop(nofuse=True)
                        sp.dma_start(ebuf[:, k, :], io["edge_attr_256"][bass.ds(e, P), :]).then_inc(s_egath[k], 16)

            def read_table(q):
                r = READS_TABLE.index(DENSE[q])
                sp.wait_ge(s_tabst, 16 * PIECES * (1 + [0, 1, 3][r]))
                with sp.Fori(0, BI) as i:
                    for j in range(2):
                        sp.wait_ge(s_op, i * 2 + (NB * q + j + 1))
                        sp.dma_start(tin[:, j, :], table_b[:, bass.ds(i * 2 + j, 1), :].rearrange("p b d -> p (b d)")
                                     ).then_inc(s_tin[j], 16)

            store_table(s_row, 2)
            sp.wait_ge(s_batchnorms, 1)
            read_table(0)
            store_table(s_done, 2)
            read_table(1)
            store_table(s_row, 2 + NB)
            for h in range(2):
                sp.wait_ge(s_scat[1][h], 16 * GROUP * STEPS)
            sp.wait_ge(s_blkst[1], 16)
            load_records(1)
            for k, a in (("L1", io["L1_gnn_W"]), ("L1a", io["L1_gnn_W1"]), ("L1b", io["L1_gnn_W2"]),
                         ("L2a", io["L2_gnn_W1"]), ("L2b", io["L2_gnn_W2"]),
                         ("L3a", io["L3_gnn_W1"]), ("L3b", io["L3_gnn_W2"])):
                sp.dma_start(W[k], a.rearrange("(k p) n -> p k n", p=P)).then_inc(s_late, 16)
            sp.wait_ge(s_added, T * 3 + BANKS)
            load_records(0)
            store_table(s_row, 2 + 2 * NB)
            mixed = sp.value_load(unsorted[0:1, 0:1], min_val=0, max_val=1)
            with sp.If(mixed < 1):
                load_edges(3)
            read_table(3)
            store_table(s_done, 2 + 4 * NB)
            store_table(s_done, 2 + 5 * NB)
            n = -(-full // 4)
            for c in range(0, full, n):
                to = min(c + n, full)
                sp.wait_ge(s_done, 2 + 6 * NB + to)
                sp.dma_start(out[c * P:to * P].rearrange("(b p) d -> p b d", p=P),
                             x_all[:, c * D:to * D].rearrange("p (b d) -> p b d", d=D)).then_inc(s_out, 16)
            if N % P:
                sp.wait_ge(s_done, 2 + 6 * NB + full + 1)
                sp.dma_start(out[full * P:N], x_all[0:N % P, full * D:(full + 1) * D]).then_inc(s_out, 16)
            sp.wait_ge(s_out, 16 * (-(-full // n) + (1 if N % P else 0)))

        @block.gpsimd
        def _(pool):
            link = Chain(pool, s_pchain)
            nc.gpsimd.iota(iota_f[:], pattern=[[1, P]], base=0, channel_multiplier=0,
                           allow_small_or_imprecise_dtypes=True)
            nc.gpsimd.iota(tile_no, pattern=[[P, TW]], base=0, channel_multiplier=1,
                           allow_small_or_imprecise_dtypes=True)
            link(nc.gpsimd.memset(ident[:], 0.0))
            link(nc.gpsimd.affine_select(out=ident[:], in_=ident[:], compare_op=ALU.not_equal, fill=1.0, base=0,
                                         pattern=[[-1, P]], channel_multiplier=1))
            link(nc.gpsimd.memset(tri[:], 0.0))
            link(nc.gpsimd.affine_select(out=tri[:], in_=tri[:], compare_op=ALU.is_ge, fill=1.0, base=0,
                                         pattern=[[-1, P]], channel_multiplier=1))
            nc.gpsimd.iota(edge_no, pattern=[[1, COLS]], base=0, channel_multiplier=COLS).then_inc(s_iota, 1)

            def scatter(i, o, h, staged):
                at = bass.ds(i * (2 * GROUP) + h * GROUP, GROUP)
                to = stage_rec[:, h, :].rearrange("p (u f) -> p u f", f=FIELDS)
                fields = (src_i, low_f, weight1, edge_no) if o == 0 else (dst1_i, low1, weight)
                for f, a in enumerate(fields):
                    nc.gpsimd.tensor_copy(to[:, :, f], a[:, at])
                nc.gpsimd.tensor_copy(stage_idx[:, h, :], (place_i, place1_i)[o][:, at]).then_inc(s_spchain[o], 1)
                pool.wait_ge(s_spchain[o], staged)
                pool.nop(nofuse=True)
                for u in range(GROUP):
                    nc.gpsimd.indirect_dma_start(
                        out=records[o][:, :], out_offset=bass.IndirectOffsetOnAxis(ap=stage_idx[:, h, u:u + 1], axis=0),
                        in_=stage_rec[:, h, u * FIELDS:(u + 1) * FIELDS], in_offset=None).then_inc(s_scat[o][h], 16)

            def scatters(o, lo, hi):
                if lo == 0:
                    for h in range(2):
                        scatter(0, o, h, h + 1)
                    lo = 1
                with pool.Fori(lo, hi) as i:
                    for h in range(2):
                        pool.wait_ge(s_scat[o][h], i * (16 * GROUP))
                        pool.nop(nofuse=True)
                        scatter(i, o, h, i * 2 + (h + 1))

            link(nc.gpsimd.memset(stage_rec[:], 0.0))
            pool.wait_ge(s_flag, 1)
            mixed = pool.value_load(unsorted[0:1, 0:1], min_val=0, max_val=1)
            with pool.If(mixed > 0):
                pool.wait_ge(s_prefill, 32)
                pool.wait_ge(s_place[0], 1)
                scatters(0, 0, STEPS)
                for h in range(2):
                    pool.wait_ge(s_scat[0][h], 16 * GROUP * STEPS)
            with pool.Else():
                pool.wait_ge(s_chunks, 16 * 9)
                pool.wait_ge(s_tiles, 1)
                for f in range(3):
                    for j in range(TW):
                        nc.gpsimd.indirect_dma_start(
                            out=run_i[f][:, j * P:(j + 1) * P], out_offset=None, in_=chunks[f][:, :],
                            in_offset=bass.IndirectOffsetOnAxis(ap=chunk_i[:, j:j + 1], axis=0)).then_inc(s_runs, 16)

            def edge_pass(m, gather_edges):
                pool.wait_ge(s_tabst, 16 * PIECES * (m + 1))
                with pool.Fori(0, ITER) as i:
                    for h in range(2):
                        pool.wait_ge(s_staged, i * 2 + (2 * ITER * m + h + 1))
                        pool.nop(nofuse=True)
                        for u in range(HALF):
                            k = h * HALF + u
                            nc.gpsimd.indirect_dma_start(
                                out=gbuf[:, k, :], out_offset=None, in_=table[:, :],
                                in_offset=bass.IndirectOffsetOnAxis(ap=idx[:, h, u:u + 1], axis=0)).then_inc(s_gath[k], 16)
                            if gather_edges:
                                nc.gpsimd.indirect_dma_start(
                                    out=ebuf[:, k, :], out_offset=None, in_=io["edge_attr_256"][:, :],
                                    in_offset=bass.IndirectOffsetOnAxis(ap=eidx[:, h, u:u + 1], axis=0)).then_inc(s_egath[k], 16)

            edge_pass(0, False)
            pool.wait_ge(s_prefill, 32)
            pool.wait_ge(s_place[1], 1)
            scatters(1, 0, PART)
            pool.wait_ge(s_deg[1], 1)
            edge_pass(1, False)
            scatters(1, PART, STEPS)
            edge_pass(2, False)
            mixed = pool.value_load(unsorted[0:1, 0:1], min_val=0, max_val=1)
            with pool.If(mixed > 0):
                edge_pass(3, True)
            with pool.Else():
                edge_pass(3, False)

            def add_term(b):
                nc.gpsimd.tensor_tensor(b.cols(x_all, D), b.cols(x_all, D), rows["be2"][:], ALU.add).then_inc(s_term, 1)

            pairs(pool, add_term)
            edge_pass(4, False)
            edge_pass(5, False)

        @block.scalar
        def _(act):
            roots = [0]

            def root(v, r):
                roots[0] += 1
                act.wait_ge(s_root_in, roots[0])
                nc.scalar.activation(r, v, ACT.Sqrt).then_inc(s_root_out, 1)

            link = Chain(act, s_achain)
            act.wait_ge(s_buckets, 1)
            with act.Fori(0, BI) as i:
                link.enter(i, 2 * 2)
                for j in range(2):
                    b = bass.ds(i * 2 + j, 1)
                    link(nc.scalar.activation(mask1, high1_b, ACT.Abs, bias=iota_f[:, b], scale=-1.0))
                    link(nc.scalar.activation(mask1, mask1, ACT.Relu, bias=ones[:, 0:1], scale=-1.0, accum_out=cnts[1][:, b]))
                link.leave(BI)

            root(root_v[:, 0:NB], root_r[:, 0:NB])

            def edge_pass(m):
                o, weighted, attrs = PASSES[m]
                act.wait_ge(s_recld, 32 * [1, 1, 2, 3, 3, 3][m])
                recs = rec[:].rearrange("p (t f) -> p t f", f=FIELDS)

                def stage(i, h):
                    act.wait_ge(s_tile, i * RING + (T * m + HALF * (h + 1)))
                    act.nop(nofuse=True)
                    at = bass.ds(i * RING + h * HALF, HALF)
                    nc.scalar.copy(idx[:, h, :], recs[:, at, 0])
                    if attrs:
                        nc.scalar.copy(eidx[:, h, :], recs[:, at, 3])
                    nc.scalar.copy(low[:, h, :].rearrange("p (t f) -> p t f", f=2), recs[:, at, 1:3]).then_inc(s_staged, 1)

                def cut_messages(i, h):
                    for u in range(HALF):
                        k = h * HALF + u
                        act.wait_ge(s_msg, i * RING + (k + 1))
                        nc.scalar.activation(gbuf[:, k, :], gbuf[:, k, :], ACT.Relu).then_inc(s_relu, 1)

                if not attrs:
                    with act.Fori(0, ITER) as i:
                        for h in range(2):
                            stage(i, h)
                    return
                stage(0, 0)
                with act.Fori(0, ITER - 1) as i:
                    stage(i, 1)
                    cut_messages(i, 0)
                    stage(i + 1, 0)
                    cut_messages(i, 1)
                stage(ITER - 1, 1)
                cut_messages(ITER - 1, 0)
                cut_messages(ITER - 1, 1)

            def norm(scale, made):
                root(root_v[:, 0:NB], root_r[:, 0:NB])

                def cut(b):
                    act.wait_ge(s_z, b + (NB * made + 1))
                    act.nop(nofuse=True)
                    nc.scalar.activation(b.cols(acc, D), normed[b.off % 4], ACT.Relu,
                                         scale=1.0 if scale is None else b.cols(scale, 1)).then_inc(s_row, 1)

                fours(act, cut)

            def dense(q):
                kind = DENSE[q]
                n = NB * q
                if kind == "last":
                    act.wait_ge(s_added, T * 6 + BANKS)

                    def cut(b):
                        act.wait_ge(s_done, b + (n + 1))
                        act.nop(nofuse=True)
                        nc.scalar.activation(fin[:, b.j, :], b.cols(acc, D), ACT.Relu, scale=b.cols(dis, 1)).then_inc(s_fin, 1)

                    pairs(act, cut)
                    return
                width = 2 * D if kind in ("gcn0", "gcn1") else D
                f = MIDDLE.index(kind) if kind in MIDDLE else None

                def turned(b):
                    act.wait_ge(s_turn, b + (n + 1))
                    nc.scalar.activation(opT[:, b.j, 0:width], bank[4 + b.j][:, 0:width],
                                         ACT.Relu if kind == "lin1" else ACT.Copy).then_inc(s_turned, 1)

                def middle_product(b):
                    act.wait_ge(s_m, b + (NB * f + 1))
                    func, bias = (ACT.Relu, "L1b1") if kind == "mlp" else (ACT.Gelu, "L2b1")
                    for c in range(KC):
                        at = slice(c * P, (c + 1) * P)
                        ins = nc.scalar.activation(mid[:, b.j, at], bank[6 + b.j][:, at], func, bias=cols[bias][:, c:c + 1])
                    ins.then_inc(s_mo, 1)

                stages = [deepest(kind)]
                if kind != "gine":
                    stages.append((TURN_LAG, turned))
                if kind in MIDDLE:
                    stages.append((MID_LAG, middle_product))
                pipeline(act, stages)

            norm(dis, 0)
            root(root_v[:, 0:KC], root_r[:, 0:KC])
            root(root_v, root_r)
            edge_pass(0)
            dense(0)
            edge_pass(1)
            dense(1)
            root(root_v[:, 0:NB], root_r[:, 0:NB])
            norm(diw, 1)
            edge_pass(2)
            dense(2)
            norm(None, 2)
            edge_pass(3)
            dense(3)
            root(root_v[:, 0:NB], root_r[:, 0:NB])
            dense(4)
            edge_pass(4)
            dense(5)
            edge_pass(5)
            dense(6)

        @block.tensor
        def _(pe):
            pe.wait_ge(s_iota, 1)
            pe.wait_ge(s_pads, 1)
            pe.wait_ge(s_viol, 1)
            nc.tensor.matmul(bank[3][:, 0:1], ones[:], cnt[:, 0:1], start=True, stop=True).then_inc(s_violsum, 1)
            pe.wait_ge(s_flag, 1)
            mixed = pe.value_load(unsorted[0:1, 0:1], min_val=0, max_val=1)
            with pe.If(mixed < 1):
                pe.wait_ge(s_rows, 1)
                for n, t in enumerate((begun, step_f)):
                    for c in range(2):
                        ins = nc.tensor.matmul(bank[4 + 2 * n + c][:, 0:HW], ones[0:1, :], t[0:1, c * HW:c * HW + HW],
                                               start=True, stop=True)
                ins.then_inc(s_rowsout, 1)

            def degrees_open(b):
                nc.tensor.matmul(b[:, 0:NB], zero[:], zero[:, 0:NB], start=True, stop=False, skip_group_check=True)

            def degrees_add(b, ohl, ohh):
                for u in range(GROUP):
                    ins = nc.tensor.matmul(b[:, 0:NB], ohl[:, u * P:(u + 1) * P], ohh[:, u * NB:(u + 1) * NB],
                                           start=False, stop=False, skip_group_check=True)
                return ins

            def degrees_close(b):
                return nc.tensor.matmul(b[:, 0:NB], zero[:], zero[:, 0:NB], start=False, stop=True, skip_group_check=True)

            def bucket_sums(o):
                if o == 0:
                    pe.wait_ge(s_cnt0, 1)
                else:
                    pe.wait_ge(s_achain, 2 * NB)
                nc.tensor.matmul(bank[2][:, 0:NB], tri[:], cnts[o], start=True, stop=True)
                nc.tensor.matmul(bank[2][:, NB:2 * NB], ones[:], cnts[o], start=True, stop=True).then_inc(s_off[o], 1)

            def degrees(o, b, ohl, ohh):
                degrees_open(b)
                with pe.Fori(0, STEPS) as i:
                    for h in range(2):
                        pe.wait_ge(s_oh[o], i * 2 + (h + 1))
                        degrees_add(b, ohl[h], ohh[h]).then_inc(s_ohused[o], 1)
                degrees_close(b).then_inc(s_deg[o], 1)

            degrees(0, bank[0], oh_low, oh_high)
            bucket_sums(1)
            with pe.If(mixed > 0):
                bucket_sums(0)
            with pe.Else():
                pe.wait_ge(s_lows, 1)
                for f, t in enumerate((run_f[0], run_f[1], run_i[2])):
                    for j in range(TW):
                        g = f * TW + j
                        ins = nc.tensor.transpose(bank[TURN[g // 4]][:, (g % 4) * P:(g % 4 + 1) * P],
                                                  t[:, j * P:(j + 1) * P], ident[:])
                ins.then_inc(s_runT, 1)

            def edge_pass(m):
                o, weighted, attrs = PASSES[m]

                with pe.Fori(0, ITER) as i:
                    for k in range(RING):
                        pe.wait_ge(s_onehot, i * RING + (T * m + k + 1))
                        if attrs:
                            pe.wait_ge(s_relu, i * RING + (k + 1))
                        else:
                            pe.wait_ge(s_gath[k], i * 16 + 16 * (ITER * m + 1))
                        pe.wait_ge(s_added, i * RING + (T * m + k + 1))
                        nc.tensor.matmul(bank[k % BANKS][:, 0:D], onehot[:, k, :], gbuf[:, k, :],
                                         start=True, stop=True).then_inc(s_tile, 1)

            def dense(q):
                kind = DENSE[q]
                if kind == "last":
                    return
                n = NB * q
                two = kind in ("gcn0", "gcn1")
                wa, wb = {"gcn0": ("L0a", "L0r"), "gcn1": ("L0b", "L0r"), "mlp": ("L1b", "L1"),
                          "gine": ("L2b", "L2a"), "lin1": ("L3a", None), "lin2": ("L3b", None)}[kind]

                def middle(to, w, of):
                    for m_ in range(KC):
                        for k in range(KC):
                            ins = nc.tensor.matmul(to[:, m_ * P:(m_ + 1) * P], W[w][:, k, m_ * P:(m_ + 1) * P],
                                                   of[:, k * P:(k + 1) * P], start=(k == 0), stop=(k == KC - 1))
                    return ins

                f = MIDDLE.index(kind) if kind in MIDDLE else None

                def turn(b):
                    pe.wait_ge(s_op, b + (n + 1 + 2))
                    for s, t in enumerate([opa, opb] if two else [opa]):
                        for c in range(KC):
                            at = (s * KC + c) * P
                            ins = nc.tensor.transpose(bank[4 + b.j][:, at:at + P], t[:, b.j, c * P:(c + 1) * P], ident[:])
                    ins.then_inc(s_turn, 1)

                def middle_product(b):
                    pe.wait_ge(s_turned, b + (n + 1))
                    middle(bank[6 + b.j], wb, opT[:, b.j, :]).then_inc(s_m, 1)

                def last(b):
                    if kind in MIDDLE:
                        pe.wait_ge(s_mo, b + (NB * f + 1))
                        src = mid
                    else:
                        pe.wait_ge(s_turned, b + (n + 1))
                        src = opT
                    if b.i is not None or b.off >= 2:
                        pe.wait_ge(s_fin, b + (n - 1))
                    ws = [wa, wb] if two else [wa]
                    for s, w in enumerate(ws):
                        for k in range(KC):
                            at = (s * KC + k) * P
                            ins = nc.tensor.matmul(bank[b.j][:, 0:D], src[:, b.j, at:at + P], W[w][:, k, :],
                                                   start=(s == 0 and k == 0),
                                                   stop=(s == len(ws) - 1 and k == KC - 1))
                    ins.then_inc(s_pf, 1)

                stages = [deepest(kind), (TURN_LAG, turn)]
                if kind in MIDDLE:
                    stages.append((MID_LAG, middle_product))
                stages.append((LAST_LAG[kind], last))
                if kind == "gine":
                    pe.wait_ge(s_folded, 1)
                pipeline(pe, stages)

            pe.wait_ge(s_params, 16 * PARAMS)
            edge_pass(0)
            dense(0)
            degrees(1, bank[7], oh1_low, oh1_high)
            edge_pass(1)
            dense(1)
            pe.wait_ge(s_late, 16 * 7)
            for k in range(KC):
                for m_ in range(KC):
                    ins = nc.tensor.transpose(bank[4][:, m_ * D + k * P:m_ * D + (k + 1) * P], W["L1"][:, k, m_ * P:(m_ + 1) * P], ident[:])
            ins.then_inc(s_foldT, 1)
            pe.wait_ge(s_foldTo, 1)
            for r in range(KC):
                for m_ in range(KC):
                    nc.tensor.matmul(bank[5][:, r * D:(r + 1) * D], opT[:, 0, m_ * D + r * P:m_ * D + (r + 1) * P], W["L1a"][:, m_, :],
                                     start=(m_ == 0), stop=(m_ == KC - 1))
            for r in range(KC):
                for k in range(KC):
                    ins = nc.tensor.matmul(bank[6][:, r:r + 1], W["L1a"][:, k, r * P:(r + 1) * P], cols["L1b"][:, k:k + 1],
                                           start=(k == 0), stop=(k == KC - 1))
            ins.then_inc(s_foldP, 1)
            edge_pass(2)
            pe.wait_ge(s_mlp, 1)
            dense(2)
            edge_pass(3)
            dense(3)
            dense(4)
            edge_pass(4)
            dense(5)
            edge_pass(5)

        @block.vector
        def _(dve):
            link = Chain(dve, s_chain)
            V = nc.vector
            roots = [0]

            V.memset(zero[:], 0.0)
            for t in (src_i, dst_i, dst_next, dst1_i):
                V.memset(t[96:P, :], PAD_NODE)
            V.memset(pads[0], 0)
            V.memset(pads[1], -P * NB)
            V.memset(pads[2], 0.0)
            V.memset(weight1[96:P, :], 0.0)
            V.memset(weight[96:P, :], 0.0).then_inc(s_pads, 1)
            r3 = rec[:].rearrange("p (t f) -> p t f", f=FIELDS)
            link(V.memset(rec[:], 0.0))
            V.memset(r3[:, :, 1:2], -1.0).then_inc(s_unfilled, 1)
            V.memset(ones[:], 1.0).then_inc(s_ohused[0], 2)
            V.memset(tmpa[:], 0.0).then_inc(s_added, BANKS)
            V.memset(tmpb[:], 0.0).then_inc(s_row, 2)
            V.memset(mean[:], 0.0).then_inc(s_op, 2)
            V.memset(rstd[:], 0.0).then_inc(s_done, 2)
            V.memset(stats[:], 0.0).then_inc(s_ohused[1], 2)
            V.memset(x_all[:, (N // P) * D:], 0.0).then_inc(s_xfree, 1)
            dve.wait_ge(s_iota, 1)
            dve.wait_ge(s_edges, 16 * 12)

            spare_i = spare.bitcast(I32)
            link(V.tensor_scalar(spare_i, src_i, 7, None, ALU.logical_shift_right))
            V.tensor_copy(high1_b, spare_i).then_inc(s_buckets, 1)

            link(V.tensor_tensor(place, dst_i, dst_next, ALU.is_gt))
            V.tensor_reduce(cnt[:, 0:1], place, AX_X, ALU.add).then_inc(s_viol, 1)
            link(V.tensor_scalar(edge_no, edge_no, E - 1, None, ALU.min))
            dve.wait_ge(s_violsum, 1)
            V.tensor_scalar(unsorted[:], bank[3][:, 0:1], 1.0, None, ALU.min).then_inc(s_flag, 1)
            dve.wait_ge(s_flag, 1)
            mixed = dve.value_load(unsorted[0:1, 0:1], min_val=0, max_val=1)

            sl = Chain(dve, s_schain)
            dve.wait_ge(s_ends, 64)
            with dve.If(mixed < 1):
                row, begun_, step_, hit_ = place_i[0:1, :], begun[0:1, :], step_f[0:1, :], hit[0:1, :]
                sl(V.tensor_scalar(edge_ends, edge_ends, 7, None, ALU.logical_shift_right))
                sl(V.tensor_copy(begun_, edge_ends[:, 0:COLS]))
                sl(V.tensor_tensor(step_, edge_ends[:, COLS:], begun_, ALU.subtract))
                sl(V.tensor_scalar(step_, step_, 1.0, None, ALU.add))
                sl(V.tensor_tensor_scan(hit_, step_, step_, 0.0, ALU.add, ALU.max))
                sl(V.tensor_tensor(hit_, hit_, step_, ALU.subtract))
                sl(V.tensor_tensor(step_, begun_, hit_, ALU.subtract))
                sl(V.tensor_copy(place[0:1, :], step_))
                sl(V.tensor_copy(begun_, hit_))
                V.tensor_tensor(step_[:, 1:COLS], place[0:1, 1:COLS], place[0:1, 0:COLS - 1], ALU.subtract).then_inc(s_rows, 1)
            link(V.tensor_scalar(work_i, dst_i, P - 1, None, ALU.bitwise_and))
            V.tensor_copy(low_b, work_i)
            link(V.tensor_copy(low_f, work_i))
            link(V.tensor_scalar(work_i, dst_i, 7, None, ALU.logical_shift_right))
            link(V.tensor_copy(high_f, work_i))
            link(V.tensor_copy(iota_b[:], iota_f[:]))
            link(V.tensor_copy(high_b, work_i))
            link(V.tensor_scalar(spare_i, src_i, P - 1, None, ALU.bitwise_and))
            link(V.tensor_copy(low1, spare_i))
            with dve.If(mixed < 1):
                dve.wait_ge(s_rowsout, 1)
                for n, t in enumerate((begun, step_f)):
                    for c in range(2):
                        w = min(HW, COLS - c * HW)
                        ins = V.tensor_copy(t[:, c * HW:c * HW + w], bank[4 + 2 * n + c][:, 0:w])
                sl(ins)
                for j in range(TW):
                    sl(V.tensor_scalar(hit, begun, tile_no[:, j:j + 1], None, ALU.is_le, ALU.add, accum_out=t_chunk[:, j:j + 1]))
                    sl(V.scalar_tensor_tensor(hit, begun, tile_no[:, j:j + 1], step_f, ALU.is_le, ALU.mult,
                                              accum_out=t_block[:, j:j + 1]))
                sl(V.tensor_tensor(t_block, t_block, tile_no, ALU.add))
                sl(V.tensor_scalar(t_block, t_block, NB - 1.0, None, ALU.min))
                sl(V.tensor_scalar(t_base, t_block, float(P), None, ALU.mult))
                V.tensor_scalar(blk_i[0], t_block, float(D), None, ALU.mult)
                V.tensor_scalar(chunk_i, t_chunk, -1.0, None, ALU.add)
                sl(V.tensor_scalar(t_chunk, t_chunk, -1.0, float(P), ALU.add, ALU.mult))
                V.tensor_scalar(first_i, t_chunk, float(E - P), None, ALU.min).then_inc(s_tiles, 1)


            def onehots_of(to, values, width, i, h, iota):
                c = bass.ds(i * (2 * GROUP) + h * GROUP, GROUP)
                return V.tensor_tensor(to.rearrange("p (c n) -> p c n", n=width), iota[:, 0:width].unsqueeze(1).to_broadcast([P, GROUP, width]),
                                       values[:, c].unsqueeze(2).to_broadcast([P, GROUP, width]), ALU.is_equal)

            with dve.Fori(0, STEPS) as i:
                for h in range(2):
                    dve.wait_ge(s_ohused[0], i * 2 + (h + 1))
                    onehots_of(oh_low[h], low_b, P, i, h, iota_b)
                    onehots_of(oh_high[h], high_b, NB, i, h, iota_b).then_inc(s_oh[0], 1)

            def weighted_degrees():
                with dve.Fori(0, STEPS) as i:
                    link.enter(i, 2)
                    for h in range(2):
                        dve.wait_ge(s_ohused[1], i * 2 + (h + 1))
                        onehots_of(oh1_low[h], low1, P, i, h, iota_f)
                        link(onehots_of(oh1_high[h], high1_b, NB, i, h, iota_f))
                        high = oh1_high[h].rearrange("p (c n) -> p c n", n=NB)
                        c = bass.ds(i * (2 * GROUP) + h * GROUP, GROUP)
                        V.tensor_tensor(high, high, weight[:, c].unsqueeze(2).to_broadcast([P, GROUP, NB]), ALU.mult
                                        ).then_inc(s_oh[1], 1)
                    link.leave(STEPS)

            def bucket_counts(o, highs, junk, chain):
                with dve.Fori(0, BI) as i:
                    chain.enter(i, 2)
                    for j in range(2):
                        b = bass.ds(i * 2 + j, 1)
                        chain(V.tensor_scalar(junk, highs, iota_f[:, b], None, ALU.is_equal, ALU.add, accum_out=cnt[:, b]))
                    chain.leave(BI)
                V.memset(tmpa[:], 0.0).then_inc(s_cnt0, 1)

            def bucket_places(o, chain):
                dve.wait_ge(s_off[o], 1)
                whole_i = whole.bitcast(I32)
                chain(V.tensor_scalar(whole_i, bank[2][:, NB:2 * NB], P - 1.0, None, ALU.add))
                chain(V.tensor_scalar(whole_i, whole_i, 7, None, ALU.logical_shift_right))
                chain(V.tensor_copy(tiles, whole_i))
                chain(V.tensor_tensor_scan(ends, tiles, zero[:, 0:NB], 0.0, ALU.add, ALU.add))
                chain(V.tensor_tensor(first, ends, tiles, ALU.subtract))
                chain(V.scalar_tensor_tensor(start[o], first, float(P), bank[2][:, 0:NB], ALU.mult, ALU.add))
                cmp = blk_cmp.rearrange("p (t b) -> p t b", b=NB)[:, :, 0:NB - 1]
                chain(V.tensor_tensor(cmp, tile_no.unsqueeze(2).to_broadcast([P, TW, NB - 1]),
                                      ends[:, 0:NB - 1].unsqueeze(1).to_broadcast([P, TW, NB - 1]), ALU.is_ge))
                chain(V.tensor_reduce(blk_f, cmp, AX_X, ALU.add))
                V.tensor_scalar(blk_i[o], blk_f, float(D), None, ALU.mult).then_inc(s_blk[o], 1)

            def bucket_scan(b, highs, msk, scn, plc, first_place, chain):
                chain(V.tensor_scalar(msk, highs, iota_f[:, bass.ds(b, 1)], None, ALU.is_equal))
                chain(V.tensor_tensor_scan(scn, msk, msk, first_place[:, bass.ds(b, 1)], ALU.add, ALU.max))
                chain(V.copy_predicated(plc, msk.bitcast(U16), scn))

            def to_rows(o, plc, wrk, rows_, chain):
                chain(V.tensor_scalar(wrk, plc, -1.0, None, ALU.add))
                chain(V.tensor_scalar(rows_, wrk, P - 1, None, ALU.bitwise_and))
                chain(V.tensor_scalar(wrk, wrk, 7, None, ALU.logical_shift_right))
                V.scalar_tensor_tensor(rows_, rows_, float(T), wrk, ALU.mult, ALU.add).then_inc(s_place[o], 1)

            bucket_places(1, link)
            link(V.memset(place1, 0.0))

            def block_statistics(b):
                V.bn_stats(b.cols(stats, 6), b.cols(x_all, D))

            with dve.If(mixed < 1):
                dve.wait_ge(s_runs, 16 * 3 * TW)
                V.tensor_copy(run_f[0], run_i[0])
                for j in range(TW):
                    at = slice(j * P, (j + 1) * P)
                    ins = V.tensor_scalar(run_f[1][:, at], run_i[1][:, at], t_base[:, j:j + 1], None, ALU.subtract)
                ins.then_inc(s_lows, 1)
            dve.wait_ge(s_nodes, 32 if N % P else 16)
            pairs(dve, block_statistics)

            with dve.If(mixed > 0):
                gl = Chain(dve, s_gchain)
                bucket_counts(0, high_b, mask, gl)
                bucket_places(0, gl)
                gl(V.memset(place, 0.0))
                with dve.Fori(0, NB) as i:
                    gl.enter(i, 3)
                    bucket_scan(i, high_b, mask, scan, place, start[0], gl)
                    gl.leave(NB)
                to_rows(0, place, work_i, place_i, gl)
                dve.wait_ge(s_place[0], 1)
                dve.wait_ge(s_blkst[0], 16)
                for h in range(2):
                    dve.wait_ge(s_scat[0][h], 16 * GROUP * STEPS)
                gl(V.memset(tmpb[:], 0.0))
            with dve.Else():
                dve.wait_ge(s_runT, 1)
                dve.wait_ge(s_prefill, 32)
                for f in range(3):
                    for j in range(TW):
                        g, n = f * TW + j, min(P, T - j * P)
                        ins = V.tensor_copy(r3[:, j * P:j * P + n, f], bank[TURN[g // 4]][:, (g % 4) * P:(g % 4) * P + n])
                ins.then_inc(s_built, 1)
                dve.wait_ge(s_built, 1)
                dve.wait_ge(s_blkst[0], 32)
                sl(V.memset(tmpb[:], 0.0))

            dve.wait_ge(s_deg[0], 1)
            dve.wait_ge(s_blkst[1], 16)
            link(V.tensor_scalar(dis[:], bank[0][:, 0:NB], 1.0, None, ALU.add))
            V.memset(tmpa[:], 0.0).then_inc(s_tile, RING)

            roots = [0]

            def inverse_root(asked, w, to):
                roots[0] += 1
                asked.then_inc(s_root_in, 1)
                dve.wait_ge(s_root_out, roots[0])
                v, r, t = root_v[:, 0:w], root_r[:, 0:w], root_t[:, 0:w]
                link(V.reciprocal(r, r))
                link(V.tensor_tensor(t, v, r, ALU.mult))
                link(V.tensor_tensor(t, t, r, ALU.mult))
                link(V.tensor_scalar(t, t, -0.5, 1.5, ALU.mult, ALU.add))
                link(V.tensor_tensor(to, r, t, ALU.mult))

            inverse_root(V.tensor_copy(root_v[:, 0:NB], dis[:]), NB, dis[:])
            link(V.tensor_tensor(sq[:], root_v[:, 0:NB], dis[:], ALU.mult))

            def batchnorms():
                dve.wait_ge(s_params, 16 * PARAMS)
                inverse_root(V.tensor_scalar(root_v[:, 0:KC], cols["var1"][:], EPS, None, ALU.add), KC, cols["var1"][:])
                link(V.tensor_tensor(cols["g1"][:], cols["g1"][:], cols["var1"][:], ALU.mult))
                link(V.tensor_tensor(cols["mu1"][:], cols["mu1"][:], cols["g1"][:], ALU.mult))
                link(V.tensor_tensor(cols["be1"][:], cols["be1"][:], cols["mu1"][:], ALU.subtract))
                inverse_root(V.tensor_scalar(root_v, rows["var2"][:], EPS, None, ALU.add), D, rows["var2"][:])
                link(V.tensor_tensor(rows["g2"][:], rows["g2"][:], rows["var2"][:], ALU.mult))
                link(V.tensor_tensor(rows["L2b2"][:], rows["L2b2"][:], rows["mu2"][:], ALU.subtract))
                link(V.tensor_tensor(rows["L2b2"][:], rows["L2b2"][:], rows["g2"][:], ALU.mult))
                link(V.tensor_tensor(rows["be2"][:], rows["be2"][:], rows["L2b2"][:], ALU.add))
                link(V.tensor_tensor(rows["L0a"][:], rows["L0a"][:], rows["L0r"][:], ALU.add))
                V.tensor_tensor(rows["L0b"][:], rows["L0b"][:], rows["L0r"][:], ALU.add).then_inc(s_batchnorms, 1)

            def weighted_factors():
                dve.wait_ge(s_deg[1], 1)
                link(V.tensor_scalar(diw[:], bank[7][:, 0:NB], 1.0, None, ALU.add))
                link(V.tensor_scalar(tmpa[:], diw[:], 0.0, None, ALU.is_gt))
                inverse_root(V.tensor_scalar(root_v[:, 0:NB], diw[:], 1e-30, None, ALU.max), NB, diw[:])
                link(V.tensor_tensor(diw[:], diw[:], tmpa[:], ALU.mult))

            def statistics():
                st = stats[:].rearrange("p (b s) -> p b s", s=6)
                link(V.memset(tmpb[:], 0.0))
                link(V.tensor_tensor(tmpa[:], st[:, :, 1], st[:, :, 4], ALU.add))
                link(V.tensor_scalar(mean[:], tmpa[:], 0.5, None, ALU.mult))
                link(V.tensor_tensor(tmpa[:], st[:, :, 1], st[:, :, 4], ALU.subtract))
                link(V.scalar_tensor_tensor(tmpa[:], tmpa[:], 0.25, tmpa[:], ALU.mult, ALU.mult))
                link(V.tensor_tensor(tmpb[:], st[:, :, 2], st[:, :, 5], ALU.add))
                link(V.scalar_tensor_tensor(tmpa[:], tmpb[:], 1.0 / D, tmpa[:], ALU.mult, ALU.add))
                inverse_root(V.tensor_scalar(root_v[:, 0:NB], tmpa[:], EPS, None, ALU.add), NB, rstd[:])

            def norm(made):
                statistics()

                def normalize(b):
                    if b.i is not None or b.off >= 4:
                        dve.wait_ge(s_row, b + (NB * made - 1))
                    V.tensor_scalar(normed[b.off % 4], b.cols(x_all, D), b.cols(mean, 1), b.cols(rstd, 1),
                                    ALU.subtract, ALU.mult).then_inc(s_z, 1)

                fours(dve, normalize)

            def edge_pass(m):
                o, weighted, attrs = PASSES[m]
                dve.wait_ge(s_recld, 32 * [1, 1, 2, 3, 3, 3][m])
                dve.wait_ge(s_tabst, 16 * PIECES * (m + 1))

                def onehots(i, h):
                    dve.wait_ge(s_staged, i * 2 + (2 * ITER * m + h + 1))
                    lows = low[:, h, :].rearrange("p (t f) -> p t f", f=2)
                    if not weighted:
                        V.tensor_tensor(onehot[:, h * HALF:(h + 1) * HALF, :], iota_f[:].unsqueeze(1).to_broadcast([P, HALF, P]),
                                        lows[:, :, 0:1].to_broadcast([P, HALF, P]), ALU.is_equal).then_inc(s_onehot, HALF)
                        return
                    for u in range(HALF):
                        V.tensor_scalar(onehot[:, h * HALF + u, :], iota_f[:], lows[:, u, 0:1], lows[:, u, 1:2],
                                        ALU.is_equal, ALU.mult).then_inc(s_onehot, 1)

                def message(i, k):
                    dve.wait_ge(s_gath[k], i * 16 + 16 * (ITER * m + 1))
                    dve.wait_ge(s_egath[k], i * 16 + 16)
                    V.tensor_tensor(gbuf[:, k, :], gbuf[:, k, :], ebuf[:, k, :], ALU.add).then_inc(s_msg, 1)

                columns = [None] * LOADS

                def add(i, k):
                    if k % LOADS == 0:
                        columns[:] = load_row(row0, i * RING + k, mybir.EngineType.DVE, (NB - 1) * D)
                    to = acc[:, bass.ds(columns[k % LOADS], D)]
                    dve.wait_ge(s_tile, i * RING + (T * m + k + 1 + RING))
                    dve.wait_ge(s_added, i * RING + (T * m + k + BANKS))
                    V.tensor_tensor(to, to, bank[k % BANKS][:, 0:D], ALU.add).then_inc(s_added, 1)

                lag = LAG if attrs else 0
                turn = lag + 1
                assert turn < HALF

                def iteration(i, extra=False, begins=False, ends=False):
                    for k in range(RING):
                        if k == turn:
                            onehots(i, 1)
                        if k == 0:
                            if extra:
                                bucket_scan(i, high1_b, mask1, scan1, place1, start[1], link)
                        if k == HALF + turn and not ends:
                            onehots(i + 1, 0)
                        if attrs:
                            message(i, k)
                        if not (begins and k < lag):
                            add(i, k - lag)
                    if ends:
                        for k in range(RING - lag, RING):
                            add(i, k)

                lo = EXTRA.get(m, 0)
                onehots(0, 0)
                if lo:
                    with dve.Fori(0, lo) as i:
                        link.enter(i, 3)
                        iteration(i, extra=True)
                        link.leave(lo)
                elif lag:
                    iteration(0, begins=True)
                    lo = 1
                if lo < ITER - 1:
                    with dve.Fori(lo, ITER - 1) as i:
                        iteration(i)
                iteration(ITER - 1, ends=True)
                if m == 0:
                    to_rows(1, place1, spare_i, place1_i, link)
                    dve.wait_ge(s_place[1], 1)

            def dense(q):
                kind = DENSE[q]
                n = NB * q
                dve.wait_ge(s_batchnorms, 1)
                dve.wait_ge(s_added, T * {"gcn0": 1, "gcn1": 2, "mlp": 3, "gine": 4, "lin1": 4, "lin2": 5, "last": 6}[kind] + BANKS)
                dve.wait_ge(s_done, n + 2)
                row = {"gcn0": "L0a", "gcn1": "L0b", "mlp": "L1b2", "lin1": "L3b1", "lin2": "L3b2"}.get(kind)

                def operand(b):
                    a = b.cols(acc, D)
                    if b.i is not None or b.off >= 2:
                        dve.wait_ge(s_turn, b + (n - 1))
                    if kind in READS_TABLE:
                        before = 16 * (BI * READS_TABLE.index(kind) + 1)
                        dve.wait_ge(s_tin[b.j], before + 16 * (b.off // 2) if b.i is None else
                                    b.i * 16 + (before + 16 * (b.off // 2)))
                    if kind in ("gcn0", "gcn1"):
                        V.tensor_scalar(opa[:, b.j, :], a, b.cols(dis, 1), None, ALU.mult)
                        ins = V.tensor_scalar(opb[:, b.j, :], tin[:, b.j, :], b.cols(sq, 1), None, ALU.mult)
                    elif kind == "mlp":
                        ins = V.tensor_scalar(opa[:, b.j, :], a, b.cols(diw, 1), None, ALU.mult)
                    elif kind == "gine":
                        if b.i is not None or b.off >= 2:
                            dve.wait_ge(s_res, b + -1)
                        ins = V.tensor_tensor(opa[:, b.j, :], a, tin[:, b.j, :], ALU.add)
                    elif kind == "lin1":
                        ins = V.tensor_scalar(opa[:, b.j, :], b.cols(x_all, D), b.cols(mean, 1), b.cols(rstd, 1),
                                              ALU.subtract, ALU.mult)
                    else:
                        ins = V.tensor_scalar(opa[:, b.j, :], a, b.cols(dis, 1), 0.0, ALU.mult, ALU.max)
                    ins.then_inc(s_op, 1)

                def residual(b):
                    dve.wait_ge(s_op, b + (n + 1 + 2))
                    V.tensor_tensor(b.cols(acc, D), opa[:, b.j, :], rows["g2"][:], ALU.mult).then_inc(s_res, 1)

                def turned(b):
                    dve.wait_ge(s_turn, b + (n + 1))
                    for c in range(KC):
                        ins = V.tensor_scalar(opT[:, b.j, c * P:(c + 1) * P], bank[4 + b.j][:, c * P:(c + 1) * P],
                                              cols["g1"][:, c:c + 1], cols["be1"][:, c:c + 1], ALU.mult, ALU.add)
                    ins.then_inc(s_turned, 1)

                def take(b):
                    dve.wait_ge(s_done, b + (n + 1))
                    dve.wait_ge(s_pf, b + (n + 1))
                    if kind == "gine":
                        dve.wait_ge(s_res, b + 1)
                    V.tensor_tensor(fin[:, b.j, :], bank[b.j][:, 0:D],
                                    b.cols(acc, D) if kind == "gine" else rows[row][:], ALU.add).then_inc(s_fin, 1)

                def finish(b):
                    xb, ab = b.cols(x_all, D), b.cols(acc, D)
                    dve.wait_ge(s_fin, b + (n + 1))
                    if kind == "gine":
                        dve.wait_ge(s_term, b + 1)
                    if kind == "gcn0":
                        ins = V.tensor_scalar(ab, fin[:, b.j, :], b.cols(dis, 1), 0.0, ALU.mult, ALU.max)
                    elif kind in ("lin1", "lin2"):
                        ins = V.tensor_scalar(ab, fin[:, b.j, :], b.cols(dis, 1), None, ALU.mult)
                    elif kind == "gcn1":
                        ins = V.scalar_tensor_tensor(xb, fin[:, b.j, :], 0.0, xb, ALU.max, ALU.add)
                    else:
                        ins = V.tensor_tensor(xb, xb, fin[:, b.j, :], ALU.add)
                    ins.then_inc(s_done, 1)

                def new_statistics(b):
                    dve.wait_ge(s_done, b + (n + 1 + 2))
                    block_statistics(b)

                if kind == "last":
                    pairs(dve, finish)
                else:
                    stages = [(0, operand)]
                    if kind == "gine":
                        stages += [(TURN_LAG, turned), (TURN_LAG, residual)]
                    stages += [(LAST_LAG[kind], take), (LAST_LAG[kind] + 1, finish)]
                    if kind in WITH_STATS:
                        stages.append((LAST_LAG[kind] + 2, new_statistics))
                    pipeline(dve, stages)
                dve.wait_ge(s_done, n + NB + 2)

            def fold_batchnorm():
                dve.wait_ge(s_late, 16 * 7)
                for k in range(KC):
                    ins = V.tensor_tensor(W["L2b"][:, k, :], W["L2b"][:, k, :], rows["g2"][:], ALU.mult)
                ins.then_inc(s_folded, 1)

            norm(0)
            batchnorms()
            edge_pass(0)
            dense(0)
            weighted_degrees()
            edge_pass(1)
            dense(1)
            weighted_factors()
            norm(1)
            dve.wait_ge(s_foldT, 1)
            V.tensor_copy(opT[:, 0, :], bank[4][:, 0:KC * D]).then_inc(s_foldTo, 1)
            dve.wait_ge(s_foldP, 1)
            V.tensor_copy(W["L1"].rearrange("p k n -> p (k n)"), bank[5][:, 0:KC * D])
            V.tensor_tensor(cols["L1b1"][:], cols["L1b1"][:], bank[6][:, 0:KC], ALU.add).then_inc(s_mlp, 1)
            edge_pass(2)
            fold_batchnorm()
            dense(2)
            norm(2)
            edge_pass(3)
            dense(3)
            statistics()
            dense(4)
            edge_pass(4)
            dense(5)
            edge_pass(5)
            dense(6)


_INS = ["x", "src", "dst", "edge_attr_256", "edge_weight", "edge_weight1",
        "L0_gnn_W", "L0_gnn_b", "L0_gnn_resW", "L0_gnn_resb",
        "L1_gnn_W", "L1_gnn_b", "L1_gnn_W1", "L1_gnn_b1", "L1_gnn_W2", "L1_gnn_b2",
        "L2_gnn_W1", "L2_gnn_b1", "L2_gnn_W2", "L2_gnn_b2",
        "L2_gnn_bn1_gamma", "L2_gnn_bn1_beta", "L2_gnn_bn1_mean", "L2_gnn_bn1_var",
        "L2_gnn_bn2_gamma", "L2_gnn_bn2_beta", "L2_gnn_bn2_mean", "L2_gnn_bn2_var",
        "L3_gnn_W1", "L3_gnn_b1", "L3_gnn_W2", "L3_gnn_b2"]
_TURNED = ("L2_gnn_W1", "L2_gnn_W2", "L3_gnn_W1", "L3_gnn_W2")


def kernel(**inputs):
    import numpy as np
    import concourse.bacc as bacc
    from concourse.bass_utils import run_bass_kernel_spmd

    nc = bacc.Bacc("TRN2", target_bir_lowering=False, num_devices=1)
    arrays, io = {}, {}
    for name in _INS:
        a = np.asarray(inputs[name])
        a = np.ascontiguousarray(a.T if name in _TURNED else a)
        arrays[f"in_{name}"] = a
        io[name] = nc.dram_tensor(f"in_{name}", a.shape, mybir.dt.from_np(a.dtype), kind="ExternalInput").ap()
    out = nc.dram_tensor("out_0", io["x"].shape, F32, kind="ExternalOutput").ap()
    build(nc, io, out)
    r = run_bass_kernel_spmd(nc, [arrays], core_ids=[0])
    return r.results[0]["out_0"]
```
